# Optimizing a Trainium2 kernel written in Bass

```python
import numpy as np
import jax
import jax.numpy as jnp

def _softmax(x, axis=-1):
    return jax.nn.softmax(x, axis=axis)
def _gelu(x):
    return jax.nn.gelu(x, approximate=True)
def _silu(x):
    return jax.nn.silu(x)
def _sigmoid(x):
    return jax.nn.sigmoid(x)
def _layernorm(x, axis=-1, eps=1e-5):
    m = jnp.mean(x, axis=axis, keepdims=True)
    v = jnp.var(x, axis=axis, keepdims=True)
    return (x - m) / jnp.sqrt(v + eps)
def _scatter_add(tgt, idx, src, axis=0):
    return tgt.at[idx].add(src)
def _segment_sum(src, seg, n):
    return jax.ops.segment_sum(src, seg, n)

kernel_name = 'mk_adj_resnorm_d4_adj_256_21de09'

def setup_inputs(seed: int = 0):
    np.random.seed(seed)
    _w = jnp.asarray
    def _rec_inputs():
        import jax
        import jax.numpy as jnp
        _gk = jax.random.key(seed)
        x = -0.0005146 + 1 * jax.random.normal(jax.random.fold_in(_gk, 1), (8, 2048, 256), jnp.float32)
        _a = jax.random.bernoulli(jax.random.fold_in(_gk, 2), 0.0078125, (8, 2048, 2048))
        adj = _a.astype(jnp.int32)
        return x, adj
    x, adj = _rec_inputs()
    def _L0_gnn_setup():
        import jax, jax.numpy as jnp
        import numpy as np
        B, N, C, OUT, S = (4, 2048, 256, 256, 25)
        DENSITY = 0.008
        key = jax.random.key(seed)
        kA, kX, kW = jax.random.split(key, 3)
        A = jax.random.bernoulli(kA, DENSITY, (B, N, N)).astype(jnp.int32)
        X = jax.random.normal(kX, (B, N, C), dtype=jnp.float32)
        W = jax.random.normal(kW, (2 * C, OUT), dtype=jnp.float32) * np.float32(1.0 / np.sqrt(2 * C))
        b = jnp.zeros((OUT,), dtype=jnp.float32)
        return {'A': A, 'X': X, 'W': W, 'b': b}
    _L0_gnn_all = _L0_gnn_setup()
    _L0_gnn_in = {k: v for k, v in _L0_gnn_all.items() if k in ('W', 'b', )}
    del _L0_gnn_all

    def _L1_gnn_setup():
        import jax, jax.numpy as jnp
        import numpy as np
        NEG_SLOPE = 0.2
        key = jax.random.key(seed)
        k1, k2, k3, k4 = jax.random.split(key, 4)
        B, N, Fin, Fout = (8, 2048, 256, 256)
        x = jax.random.normal(k1, (B, N, Fin), dtype=jnp.float32)
        A = jax.random.randint(k2, (B, N, N), 0, 2, dtype=jnp.int32)
        W = jax.random.normal(k3, (Fin, Fout), dtype=jnp.float32) * (1.0 / np.sqrt(Fin))
        a = jax.random.normal(k4, (2 * Fout,), dtype=jnp.float32)
        return {'x': x, 'A': A, 'W': W, 'a': a}
    _L1_gnn_all = _L1_gnn_setup()
    _L1_gnn_in = {k: v for k, v in _L1_gnn_all.items() if k in ('W', 'a', )}
    del _L1_gnn_all

    def _L2_gnn_setup():
        import jax, jax.numpy as jnp
        import numpy as np
        B, N, IN_F, OUT_F, H, NUM_EDGE_TYPES = (16, 512, 256, 256, 8, 50)
        HEAD_DIM = OUT_F // H
        LN_EPS = 1e-05
        key = jax.random.key(seed)
        ks = jax.random.split(key, 8)
        x = jax.random.normal(ks[0], (B, N, IN_F), dtype=jnp.float32)
        adj = jax.random.randint(ks[1], (B, N, N), 0, 2, dtype=jnp.int32)
        edge_types = jax.random.randint(ks[2], (B, N, N), 0, NUM_EDGE_TYPES, dtype=jnp.int32)
        W = jax.random.normal(ks[3], (IN_F, OUT_F), dtype=jnp.float32) / np.sqrt(IN_F)
        a1 = jax.random.normal(ks[4], (HEAD_DIM,), dtype=jnp.float32) / np.sqrt(HEAD_DIM)
        a2 = jax.random.normal(ks[5], (HEAD_DIM,), dtype=jnp.float32) / np.sqrt(HEAD_DIM)
        edge_emb = jax.random.normal(ks[6], (NUM_EDGE_TYPES, H), dtype=jnp.float32) * 0.02
        edge_emb = edge_emb.at[0].set(0.0)
        ln_gamma = jnp.ones((OUT_F,), dtype=jnp.float32)
        ln_beta = jnp.zeros((OUT_F,), dtype=jnp.float32)
        return {'x': x, 'adj': adj, 'edge_types': edge_types, 'W': W, 'a1': a1, 'a2': a2, 'edge_emb': edge_emb, 'ln_gamma': ln_gamma, 'ln_beta': ln_beta}
    _L2_gnn_all = _L2_gnn_setup()
    _L2_gnn_in = {k: v for k, v in _L2_gnn_all.items() if k in ('W', 'a1', 'a2', 'edge_emb', 'ln_gamma', 'ln_beta', )}
    del _L2_gnn_all

    def _L3_gnn_setup():
        import jax, jax.numpy as jnp
        import numpy as np
        B, N, IN_F, OUT_F = (32, 1024, 256, 256)
        ALPHA = 0.2
        NEG_INF = -9000000000000000.0
        key = jax.random.key(seed)
        k1, k2, k3, k4 = jax.random.split(key, 4)
        h = jax.random.normal(k1, (B, N, IN_F), dtype=jnp.float32)
        adj = jax.random.randint(k2, (B, N, N), 0, 2, dtype=jnp.int32)
        W = jax.random.normal(k3, (OUT_F, IN_F), dtype=jnp.float32) * 0.05
        a = jax.random.normal(k4, (1, 2 * OUT_F), dtype=jnp.float32) * 0.05
        return {'h': h, 'adj': adj, 'W': W, 'a': a}
    _L3_gnn_all = _L3_gnn_setup()
    _L3_gnn_in = {k: v for k, v in _L3_gnn_all.items() if k in ('W', 'a', )}
    del _L3_gnn_all

    return {
        "x": x,
        "adj": adj,
        "L0_gnn_W": _L0_gnn_in["W"],
        "L0_gnn_b": _L0_gnn_in["b"],
        "L1_gnn_W": _L1_gnn_in["W"],
        "L1_gnn_a": _L1_gnn_in["a"],
        "L2_gnn_W": _L2_gnn_in["W"],
        "L2_gnn_a1": _L2_gnn_in["a1"],
        "L2_gnn_a2": _L2_gnn_in["a2"],
        "L2_gnn_edge_emb": _L2_gnn_in["edge_emb"],
        "L2_gnn_ln_gamma": _L2_gnn_in["ln_gamma"],
        "L2_gnn_ln_beta": _L2_gnn_in["ln_beta"],
        "L3_gnn_W": _L3_gnn_in["W"],
        "L3_gnn_a": _L3_gnn_in["a"],
    }

def reference(x, adj, L0_gnn_W, L0_gnn_b, L1_gnn_W, L1_gnn_a, L2_gnn_W, L2_gnn_a1, L2_gnn_a2, L2_gnn_edge_emb, L2_gnn_ln_gamma, L2_gnn_ln_beta, L3_gnn_W, L3_gnn_a):
    import jax
    import jax.numpy as jnp
    def _L0_gnn_ref(A, X, W, b):
        import jax, jax.numpy as jnp
        import numpy as np
        B, N, C, OUT, S = (4, 2048, 256, 256, 25)
        DENSITY = 0.008
        mask = A != 0
        neg_inf = jnp.float32(-jnp.inf)
        pri = -jnp.arange(N, dtype=jnp.float32)
        scores = jnp.where(mask, pri, neg_inf)
        vals, idx = jax.lax.top_k(scores, S)
        valid = vals > neg_inf
        feats = jax.vmap(lambda x, i: x[i])(X, idx)
        feats = jnp.where(valid[..., None], feats, neg_inf)
        agg = feats.max(axis=2)
        degree = mask.sum(axis=-1)
        agg = jnp.where((degree <= S)[..., None], jnp.maximum(agg, 0.0), agg)
        h = jnp.concatenate([X, agg], axis=-1)
        out = jax.nn.relu(jnp.einsum('bnf,fo->bno', h, W) + b)
        return out

    def _L1_gnn_ref(x, A, W, a):
        import jax, jax.numpy as jnp
        import numpy as np
        NEG_SLOPE = 0.2
        h = jnp.einsum('bnf,fd->bnd', x, W)
        d = h.shape[-1]
        s_src = h @ a[:d]
        s_dst = h @ a[d:]
        e = s_src[:, :, None] + s_dst[:, None, :]
        e = jnp.where(e >= 0, e, NEG_SLOPE * e)
        e = jnp.where(A <= 0, -jnp.inf, e)
        alpha = jax.nn.softmax(e, axis=-1)
        y = jnp.einsum('bij,bjd->bid', alpha, h)
        return y

    def _L2_gnn_ref(x, adj, edge_types, W, a1, a2, edge_emb, ln_gamma, ln_beta):
        import jax, jax.numpy as jnp
        import numpy as np
        B, N, IN_F, OUT_F, H, NUM_EDGE_TYPES = (16, 512, 256, 256, 8, 50)
        HEAD_DIM = OUT_F // H
        LN_EPS = 1e-05
        Bx, Nx, _ = x.shape
        Wh = (x @ W).reshape(Bx, Nx, H, HEAD_DIM)
        s1 = jnp.einsum('bnhd,d->bnh', Wh, a1)
        s2 = jnp.einsum('bnhd,d->bnh', Wh, a2)
        e = s1[:, :, None, :] + s2[:, None, :, :] + edge_emb[edge_types]
        e = jnp.where(e > 0, e, 0.2 * e)
        e = jnp.where((adj == 0)[..., None], jnp.float32(-1000000000.0), e)
        alpha = jax.nn.softmax(e, axis=2)
        h = jnp.einsum('bijh,bjhd->bihd', alpha, Wh).reshape(Bx, Nx, OUT_F)
        mu = jnp.mean(h, axis=-1, keepdims=True)
        var = jnp.mean(jnp.square(h - mu), axis=-1, keepdims=True)
        hn = (h - mu) * jax.lax.rsqrt(var + LN_EPS) * ln_gamma + ln_beta
        return jax.nn.elu(hn)

    def _L3_gnn_ref(h, adj, W, a):
        import jax, jax.numpy as jnp
        import numpy as np
        B, N, IN_F, OUT_F = (32, 1024, 256, 256)
        ALPHA = 0.2
        NEG_INF = -9000000000000000.0
        Wh = jnp.einsum('bni,oi->bno', h, W)
        a1 = a[0, :OUT_F]
        a2 = a[0, OUT_F:]
        si = Wh @ a1
        sj = Wh @ a2
        e = jax.nn.leaky_relu(si[:, :, None] + sj[:, None, :], negative_slope=ALPHA)
        attention = jnp.where(adj > 0, e, NEG_INF)
        attention = jax.nn.softmax(attention, axis=-1)
        h_prime = jnp.einsum('bij,bjo->bio', attention, Wh)
        return jax.nn.elu(h_prime)

    x = _layernorm(x + _L0_gnn_ref(adj, x, L0_gnn_W, L0_gnn_b), axis=-1)
    x = _layernorm(x + _L1_gnn_ref(x, adj, L1_gnn_W, L1_gnn_a), axis=-1)
    x = _layernorm(x + _L2_gnn_ref(x, adj, adj, L2_gnn_W, L2_gnn_a1, L2_gnn_a2, L2_gnn_edge_emb, L2_gnn_ln_gamma, L2_gnn_ln_beta), axis=-1)
    x = _layernorm(x + _L3_gnn_ref(x, adj, L3_gnn_W, L3_gnn_a), axis=-1)
    return x


_drawn_inputs = setup_inputs


def setup_inputs(seed=0):
    import zlib

    import numpy as np

    out = dict(_drawn_inputs(seed))
    spreads = {'L0_gnn_b': (0.0, 0.1), 'L2_gnn_ln_gamma': (1.0, 0.2), 'L2_gnn_ln_beta': (0.0, 0.1)}
    factors = {'L2_gnn_edge_emb': 26.143}
    for name, (base, spread) in spreads.items():
        noise = np.random.default_rng([zlib.crc32(name.encode()), seed]).standard_normal(out[name].shape)
        drawn = base * np.exp(spread * noise) if base else spread * noise
        out[name] = jnp.asarray(drawn.astype(out[name].dtype))
    for name, factor in factors.items():
        out[name] = (out[name] * factor).astype(out[name].dtype)
    return out
```

```python
from contextlib import ExitStack

import numpy as np

import concourse.bass as bass
from concourse import mybir

F32 = mybir.dt.float32
F32R = mybir.dt.float32r
F16 = mybir.dt.float16
BF16 = mybir.dt.bfloat16
I32 = mybir.dt.int32
U8 = mybir.dt.uint8
ALU = mybir.AluOpType
ACT = mybir.ActivationFunctionType
AX = mybir.AxisListType

P = 128
SLOTS = 25
ROUNDS = 4
LN_EPS = 1e-5
BIG = 3.0e38
POS_SHIFT = 60.0
NEG_SHIFT = 20.0
NEG_SLOPE = 0.2
PARTS = 3
RING = 8
IG = 512
HPAD = 32


def four_layer_graph_kernel(nc, x, adj, w0, b0, w1, a1, w2, a2s, a2d, emb, gamma, beta, w3, a3, out):
    B, N, C = x.shape
    NT = N // P
    NC = C // P
    HD = a2s.shape[0]
    H2 = C // HD
    NIG = N // IG
    TPG = IG // P
    ROWS = B * NT
    GATHERS = SLOTS

    x_rows = x.rearrange("b n c -> (b n) c")
    adj_rows = adj.rearrange("b n m -> (b n) m")
    out_rows = out.rearrange("b n c -> (b n) c")

    with ExitStack() as ctx:
        def sb(name, shape, dt):
            return ctx.enter_context(nc.sbuf_tensor(name, shape, dt))

        def psum(name, shape, dt):
            return ctx.enter_context(nc.psum_tensor(name, shape, dt))

        def sem(name):
            return ctx.enter_context(nc.semaphore(name))

        x1_dram = nc.dram_tensor("x1_scratch", (B * N, C), F32, kind="Internal").ap()
        at_dram = nc.dram_tensor("at_scratch", (B * NT * P, N), U8, kind="Internal").ap()
        s_dram = nc.dram_tensor("s_scratch", (B * 3 * H2, N), F32, kind="Internal").ap()

        ident = sb("ident", [P, P], F32)
        ident_bf = sb("ident_bf", [P, P], BF16)
        countdown = sb("countdown", [P, N], F16)
        w0_sb = sb("w0_sb", [P, 2 * NC, C], F32)
        b0_bc = sb("b0_bc", [P, C], F32)
        w_ext = [sb(f"w_ext{l}", [P, NC, C + 2 * h], F32) for l, h in ((1, 1), (2, H2), (3, 1))]
        w_row = [sb(f"w_row{l}", [P, NC, HPAD + h], F32) for l, h in ((1, 1), (2, H2), (3, 1))]
        emb_bc = sb("emb_bc", [P, H2], F32)
        emb_col = sb("emb_col", [HPAD + H2, 1], F32)
        gamma_bc = sb("gamma_bc", [P, C], F32)
        beta_bc = sb("beta_bc", [P, C], F32)
        pos_bias = sb("pos_bias", [P, 1], F32)
        neg_bias = sb("neg_bias", [P, 1], F32)
        row_bias = sb("row_bias", [P, 1], F32)
        minus_half = sb("minus_half", [P, TPG], F32)

        ps = [psum(f"ps{i}", [P, 512], F32) for i in range(8)]
        acc = ps[0:4]
        xt_ps = ps[4:6]
        pj_ps = ps[6:8]
        at_ps = [ps[i][:, :].bitcast(BF16) for i in (0, 1)]

        with ExitStack() as tmp:
            def tsb(name, shape, dt):
                return tmp.enter_context(nc.sbuf_tensor(name, shape, dt))
            a_bc = {k: tsb(f"abc_{k}", [P, n], F32) for k, n in (("1s", C), ("1d", C), ("2s", HD), ("2d", HD), ("3s", C), ("3d", C))}
            w3_in = tsb("w3_in", [P, NC, C], F32)
            prod = tsb("prod", [P, NC, C], F32)
            s_load = tmp.enter_context(nc.semaphore("s_load"))
            s_id = tmp.enter_context(nc.semaphore("s_id"))
            s_w3 = tmp.enter_context(nc.semaphore("s_w3"))
            s_step = tmp.enter_context(nc.semaphore("s_step"))
            loads = [
                (w0_sb[:, :, :], w0.rearrange("(k p) n -> p k n", p=P)),
                (w_ext[0][:, :, 0:C], w1.rearrange("(k p) n -> p k n", p=P)),
                (w_ext[1][:, :, 0:C], w2.rearrange("(k p) n -> p k n", p=P)),
                (w3_in[:, :, :], w3.rearrange("(k p) n -> p k n", p=P)),
                (b0_bc[:, :], b0.partition_broadcast(P)),
                (gamma_bc[:, :], gamma.partition_broadcast(P)),
                (beta_bc[:, :], beta.partition_broadcast(P)),
                (a_bc["1s"][:, :], a1[0:C].partition_broadcast(P)),
                (a_bc["1d"][:, :], a1[C:2 * C].partition_broadcast(P)),
                (a_bc["2s"][:, :], a2s.partition_broadcast(P)),
                (a_bc["2d"][:, :], a2d.partition_broadcast(P)),
                (a_bc["3s"][:, :], a3[0, 0:C].partition_broadcast(P)),
                (a_bc["3d"][:, :], a3[0, C:2 * C].partition_broadcast(P)),
                (emb_bc[:, :], emb[1, :].partition_broadcast(P)),
                (emb_col[HPAD:HPAD + H2, :], emb[1:2, :].rearrange("o h -> h o")),
            ]
            with nc.Block() as block0:
                @block0.sync
                def _(sp):
                    with nc.allow_non_contiguous_dma(reason="eight numbers, one to a partition"):
                        for dst, src in loads:
                            sp.dma_start(dst, src).then_inc(s_load, 16)

                @block0.gpsimd
                def _(pool):
                    nc.gpsimd.iota(countdown[:, :], pattern=[[-1, N]], base=N, channel_multiplier=0,
                                   allow_small_or_imprecise_dtypes=True)
                    nc.gpsimd.memset(minus_half[:, :], -0.5)
                    nc.gpsimd.memset(pos_bias[:, :], POS_SHIFT)
                    nc.gpsimd.memset(neg_bias[:, :], -NEG_SHIFT)
                    nc.gpsimd.memset(row_bias[:, :], POS_SHIFT + NEG_SHIFT)
                    nc.gpsimd.memset(ident[:, :], 0.0).then_inc(s_id, 1)
                    pool.wait_ge(s_id, 1)
                    nc.gpsimd.affine_select(out=ident[:, :], in_=ident[:, :], compare_op=ALU.not_equal, fill=1.0,
                                            base=0, pattern=[[-1, P]], channel_multiplier=1).then_inc(s_id, 1)
                    pool.wait_ge(s_id, 2)
                    nc.gpsimd.tensor_copy(ident_bf[:, :], ident[:, :])

                @block0.tensor
                def _(pe):
                    pe.wait_ge(s_id, 2)
                    pe.wait_ge(s_load, 16 * len(loads))
                    for k in range(NC):
                        for o in range(NC):
                            mm = nc.tensor.transpose(ps[k][:, o * P:(o + 1) * P], w3_in[:, o, k * P:(k + 1) * P], ident[:, :])
                    mm.then_inc(s_w3, 1)

                @block0.vector
                def _(dve):
                    v = nc.vector
                    for l in range(3):
                        v.memset(w_row[l][:, :, :], 0.0)
                    dve.wait_ge(s_load, 16 * len(loads))
                    dve.wait_ge(s_w3, 1)
                    for k in range(NC):
                        v.tensor_copy(w_ext[2][:, k, 0:C], ps[k][:, 0:C])
                    dve.drain()
                    for l, H, ends in ((0, 1, ("1d", "1s")), (1, H2, ("2d", "2s")), (2, 1, ("3d", "3s"))):
                        for e, end in enumerate(ends):
                            for k in range(NC):
                                pv = prod[:, k, :].rearrange("p (h d) -> p h d", h=H)
                                v.tensor_tensor(pv, w_ext[l][:, k, 0:C].rearrange("p (h d) -> p h d", h=H),
                                                a_bc[end][:, :].unsqueeze(1).to_broadcast([P, H, C // H]), ALU.mult)
                            dve.drain()
                            for k in range(NC):
                                pv = prod[:, k, :].rearrange("p (h d) -> p h d", h=H)
                                v.tensor_reduce(w_ext[l][:, k, C + e * H:C + (e + 1) * H], pv, AX.X, ALU.add)
                            dve.drain()
                            for k in range(NC):
                                v.tensor_copy(w_row[l][:, k, e * HPAD:e * HPAD + H], w_ext[l][:, k, C + e * H:C + (e + 1) * H])
                            dve.drain()

        stage_a = ctx.enter_context(ExitStack())
        def sb(name, shape, dt):
            return stage_a.enter_context(nc.sbuf_tensor(name, shape, dt))

        a_int = sb("a_int", [P, N], I32)
        a_bf = sb("a_bf", [P, N], BF16)
        prio = sb("prio", [P, N], F16)
        top = sb("top", [P, 8 * ROUNDS], F32)
        pad = sb("pad", [P, 8 * ROUNDS], F32)
        idx = sb("idx", [P, 8 * ROUNDS], I32)
        clamp = sb("clamp", [P, 4, 2], F32)
        base = sb("base", [P, 1], F32)
        nbr = sb("nbr", [P, SLOTS, C], F32)
        at_stage = sb("at_stage", [P, N], U8)
        x_in = sb("x_in", [P, C], F32)
        agg = sb("agg", [P, C], F32)
        hT = sb("hT", [P, 2 * NC, P], F32)
        y0 = sb("y0", [P, C], F32)
        st0 = sb("st0", [P, 6], F32)
        mv0 = sb("mv0", [P, 2], F32)
        rs0 = sb("rs0", [P, 1], F32)


        block = stage_a.enter_context(nc.Block())

        s_adj = sem("s_adj")
        s_xin = sem("s_xin")
        s_bf = sem("s_bf")
        s_at_ps = sem("s_at_ps")
        s_at_sb = sem("s_at_sb")
        s_at_out = sem("s_at_out")
        s_idx = sem("s_idx")
        s_gath = sem("s_gath")
        s_red = sem("s_red")
        s_agg = sem("s_agg")
        s_hT_ps = sem("s_hT_ps")
        s_hT = sem("s_hT")
        s_y0 = sem("s_y0")
        s_var0 = sem("s_var0")
        s_rs0 = sem("s_rs0")
        s_x1 = sem("s_x1")
        s_x1_out = sem("s_x1_out")

        @block.sync
        def _(sp):
            with nc.sync.Fori(0, B) as b, nc.sync.Fori(0, NT) as i:
                t = b * NT + i
                sp.wait_ge(s_bf, t + 1)
                sp.nop(nofuse=True)
                sp.dma_start(a_int[:, :], adj_rows[bass.ds(t * P, P), :]).then_inc(s_adj, 16)
                sp.wait_ge(s_x1, t + 1)
                sp.nop(nofuse=True)
                sp.dma_start(x_in[:, :], x_rows[bass.ds(t * P, P), :]).then_inc(s_xin, 16)
                sp.wait_ge(s_at_sb, 2 * t + 2)
                sp.nop(nofuse=True)
                sp.dma_start(at_dram[bass.ds(t * P, P), :], at_stage[:, :]).then_inc(s_at_out, 16)
                sp.wait_ge(s_x1, t + 2)
                sp.nop(nofuse=True)
                sp.dma_start(x1_dram[bass.ds(t * P, P), :], y0[:, :]).then_inc(s_x1_out, 16)
            sp.wait_ge(s_at_out, 16 * (ROWS + 1))
            sp.wait_ge(s_x1_out, 16 * (ROWS + 1))

        @block.gpsimd
        def _(pool):
            with nc.gpsimd.Fori(0, B) as b, nc.gpsimd.Fori(0, NT) as i:
                t = b * NT + i
                pool.wait_ge(s_idx, t + 2)
                pool.nop(nofuse=True)
                pool.wait_ge(s_red, t + 1)
                pool.nop(nofuse=True)
                for k in range(SLOTS):
                    nc.gpsimd.indirect_dma_start(
                        out=nbr[:, k, :], out_offset=None, in_=x_rows,
                        in_offset=bass.IndirectOffsetOnAxis(ap=idx[:, k:k + 1], axis=0)).then_inc(s_gath, 16)
                pool.wait_ge(s_var0, t + 1)
                pool.nop(nofuse=True)
                nc.gpsimd.tensor_tensor(rs0[:, :], mv0[:, 1:2], minus_half[:, 0:1], ALU.pow).then_inc(s_rs0, 1)

        @block.scalar
        def _(act):
            act.sem_inc(s_bf, 1)
            act.sem_inc(s_at_out, 16)
            with nc.scalar.Fori(0, B) as b, nc.scalar.Fori(0, NT) as i:
                t = b * NT + i
                act.wait_ge(s_at_ps, 2 * t + 2)
                act.nop(nofuse=True)
                act.wait_ge(s_idx, t + 1)
                act.nop(nofuse=True)
                act.wait_ge(s_adj, 16 * t + 16)
                act.nop(nofuse=True)
                nc.scalar.copy(a_bf[:, :], a_int[:, :]).then_inc(s_bf, 1)
                act.wait_ge(s_at_out, 16 * t + 16)
                act.nop(nofuse=True)
                for q in range(2):
                    act.wait_ge(s_at_ps, 2 * t + 3 + q)
                    act.nop(nofuse=True)
                    nc.scalar.copy(at_stage[:, q * 1024:(q + 1) * 1024], at_ps[q][:, 0:1024]).then_inc(s_at_sb, 1)
                act.wait_ge(s_hT_ps, t + 1)
                act.nop(nofuse=True)
                nc.scalar.copy(hT[:, :, :].rearrange("p k n -> p (k n)"), xt_ps[0][:, :]).then_inc(s_hT, 1)

        @block.tensor
        def _(pe):
            pe.sem_inc(s_at_ps, 2)
            with nc.tensor.Fori(0, B) as b, nc.tensor.Fori(0, NT) as i:
                t = b * NT + i
                pe.wait_ge(s_bf, t + 2)
                pe.nop(nofuse=True)
                for q in range(2):
                    for k in range(8):
                        j = q * 8 + k
                        mm = nc.tensor.transpose(at_ps[q][:, k * P:(k + 1) * P], a_bf[:, j * P:(j + 1) * P], ident_bf[:, :])
                    mm.then_inc(s_at_ps, 1)
                pe.wait_ge(s_xin, 16 * t + 16)
                pe.nop(nofuse=True)
                pe.wait_ge(s_agg, t + 1)
                pe.nop(nofuse=True)
                for k in range(2 * NC):
                    src = x_in if k < NC else agg
                    c = k % NC
                    mm = nc.tensor.transpose(xt_ps[0][:, k * P:(k + 1) * P], src[:, c * P:(c + 1) * P], ident[:, :])
                mm.then_inc(s_hT_ps, 1)
                pe.wait_ge(s_hT, t + 1)
                pe.nop(nofuse=True)
                for k in range(2 * NC):
                    mm = nc.tensor.matmul(pj_ps[0][:, 0:C], hT[:, k, :], w0_sb[:, k, :],
                                          start=(k == 0), stop=(k == 2 * NC - 1))
                mm.then_inc(s_y0, 1)

        @block.vector
        def _(dve):
            v = nc.vector
            dve.sem_inc(s_idx, 1)
            dve.sem_inc(s_red, 1)
            dve.sem_inc(s_x1, 1)
            dve.sem_inc(s_x1_out, 16)
            v.memset(base[:, :], -float(N))
            dve.drain()
            with nc.vector.Fori(0, B) as b:
              v.tensor_scalar(base[:, :], base[:, :], float(N), None, ALU.add)
              dve.drain()
              with nc.vector.Fori(0, NT) as i:
                t = b * NT + i
                dve.wait_ge(s_bf, t + 2)
                dve.nop(nofuse=True)
                v.tensor_tensor(prio[:, :], a_bf[:, :], countdown[:, :], ALU.mult)
                dve.drain()
                for r in range(ROUNDS):
                    v.max(top[:, 8 * r:8 * r + 8], prio[:, :])
                    dve.drain()
                    if r < ROUNDS - 1:
                        v.match_replace(prio[:, :], top[:, 8 * r:8 * r + 8], prio[:, :], 0.0)
                        dve.drain()
                v.tensor_scalar(clamp[:, 0, 0:1], top[:, 0:1], 0.0, BIG, ALU.is_gt, ALU.mult)
                v.tensor_scalar(clamp[:, 0, 1:2], top[:, SLOTS:SLOTS + 1], 0.0, -BIG, ALU.is_gt, ALU.mult)
                v.tensor_scalar(pad[:, :], top[:, :], 0.0, top[:, 0:1], ALU.is_equal, ALU.mult)
                dve.drain()
                v.tensor_tensor(pad[:, :], pad[:, :], top[:, :], ALU.add)
                dve.drain()
                v.tensor_scalar(pad[:, :], pad[:, :], -1.0, float(N), ALU.mult, ALU.add)
                dve.drain()
                v.tensor_scalar(pad[:, :], pad[:, :], float(N - 1), None, ALU.min)
                dve.drain()
                v.tensor_scalar(idx[:, :], pad[:, :], base[:, 0:1], None, ALU.add).then_inc(s_idx, 1)
                dve.wait_ge(s_gath, 16 * SLOTS * t + 16 * SLOTS)
                dve.nop(nofuse=True)
                v.tensor_reduce(agg[:, :], nbr[:, :, :].rearrange("p s c -> p c s"), AX.X, ALU.max).then_inc(s_red, 1)
                dve.drain()
                v.tensor_scalar(agg[:, :], agg[:, :], clamp[:, 0, 0:1], clamp[:, 0, 1:2], ALU.min, ALU.max).then_inc(s_agg, 1)
                dve.wait_ge(s_y0, t + 1)
                dve.nop(nofuse=True)
                dve.wait_ge(s_x1_out, 16 * t + 16)
                dve.nop(nofuse=True)
                v.tensor_tensor(y0[:, :], pj_ps[0][:, 0:C], b0_bc[:, :], ALU.add)
                dve.drain()
                v.scalar_tensor_tensor(y0[:, :], y0[:, :], 0.0, x_in[:, :], ALU.max, ALU.add)
                dve.drain()
                v.bn_stats(st0[:, :], y0[:, :])
                dve.drain()
                v.bn_aggr(mv0[:, :], st0[:, :])
                dve.drain()
                v.tensor_scalar(mv0[:, 1:2], mv0[:, 1:2], LN_EPS, None, ALU.add).then_inc(s_var0, 1)
                dve.wait_ge(s_rs0, t + 1)
                dve.nop(nofuse=True)
                v.tensor_scalar(y0[:, :], y0[:, :], mv0[:, 0:1], rs0[:, 0:1], ALU.subtract, ALU.mult).then_inc(s_x1, 1)


        stage_a.close()

        def sb(name, shape, dt):
            return ctx.enter_context(nc.sbuf_tensor(name, shape, dt))

        HW = HD + 2
        FW = C + 2
        VW = 2 * H2 * HW
        heads = (1, H2, 1)
        UNITS_A = NIG * NT
        UNITS_G = (2 * NIG * NT, NIG * NT * H2, 2 * NIG * NT)
        UNITS = sum(UNITS_G) + UNITS_A

        def shared(name, groups):
            size = max(sum(int(np.prod(shape[1:])) * 4 for _, shape in g) for g in groups)
            size = -(-size // 32) * 32
            base = -(-nc.sbuf_base // 32) * 32
            sb(name, [P, size // 4], F32)
            placed = []
            for g in groups:
                at_byte = base
                for n, shape in g:
                    placed.append(nc.alloc_sbuf_tensor_at(n, shape, F32, offset=at_byte))
                    at_byte += int(np.prod(shape[1:])) * 4
            return placed

        h_ext, tot, yy, ee, ex = shared("region_h", (
            [("h_ext", [P, NT, H2 * HW])],
            [("tot", [P, TPG, H2 * HW]), ("yy", [P, TPG, C]), ("ee", [P, TPG, C]), ("ex", [P, TPG, C])]))
        *xTc, gsb = shared("region_x", (
            [("xTc0", [P, NC, IG]), ("xTc1", [P, NC, IG])],
            [("gsb", [P, TPG, VW])]))
        *vv, avs = shared("region_v", (
            [("vv0", [P, VW]), ("vv1", [P, VW])],
            [("avs", [P, TPG, H2 * HW])]))
        xs = sb("xs", [P, NT, C], F32)
        at = sb("at", [P, NT, NT, P], U8)
        vp = sb("vp", [P, NT, 2, VW], F32R)
        sc = sb("sc", [P, NT, 2 * H2], F32)
        row_sb = [sb(f"row_sb{i}", [HPAD + H2, IG], F32) for i in range(2)]
        s1b = [sb(f"s1b{i}", [P, 4, IG], F32) for i in range(2)]
        ring = [sb(f"ring{i}", [P, IG], F32R) for i in range(RING)]
        mx4 = sb("mx4", [H2, NIG], F32)
        mx = sb("mx", [H2, 1], F32)
        mxb = sb("mxb", [H2, P], F32)
        dd = sb("dd", [P, NT, H2], F32)
        nsd = sb("nsd", [P, NT, H2], F32)
        zz = sb("zz", [P, NT, H2], F32)
        zp = sb("zp", [P, NT, H2], F32)
        v_pos = sb("v_pos", [P, NT, H2], F32)
        v_neg = sb("v_neg", [P, NT, H2], F32)
        f_pos = sb("f_pos", [P, NT, H2], F32)
        f_neg = sb("f_neg", [P, NT, H2], F32)
        rden = sb("rden", [P, TPG, H2], F32)
        st = sb("st", [P, TPG, 6], F32)
        mv = sb("mv", [P, TPG, 2], F32)
        rs = sb("rs", [P, TPG], F32)

        s_xl = sem("s_xl")
        s_atl = sem("s_atl")
        s_xT_ps = sem("s_xT_ps")
        s_xT = sem("s_xT")
        s_row_ps = sem("s_row_ps")
        s_row_sb = sem("s_row_sb")
        s_row_out = [sem(f"s_row_out{i}") for i in range(2)]
        s_h_ps = sem("s_h_ps")
        s_h = sem("s_h")
        s_mx = sem("s_mx")
        s_mx_ps = sem("s_mx_ps")
        s_cols = sem("s_cols")
        s_w = sem("s_w")
        s_vv = sem("s_vv")
        s_hi = sem("s_hi")
        s_lo = sem("s_lo")
        s_s1 = [sem(f"s_s1{i}") for i in range(2)]
        s_s1_used = [sem(f"s_s1_used{i}") for i in range(2)]
        s_mask = sem("s_mask")
        s_amask = sem("s_amask")
        s_used = sem("s_used")
        s_acc = sem("s_acc")
        s_free = sem("s_free")
        s_exp = sem("s_exp")
        s_min = sem("s_min")
        s_var = sem("s_var")
        s_rs = sem("s_rs")
        s_x = sem("s_x")
        s_gw = sem("s_gw")
        s_out = sem("s_out")

        ACCS = (2 * TPG * NIG, 3 * TPG * NIG, 2 * TPG * NIG)
        ACC0 = (0, ACCS[0], ACCS[0] + ACCS[1])
        ACC_B = sum(ACCS)
        G0 = (0, UNITS_G[0], UNITS_G[0] + UNITS_G[1])
        G_B = sum(UNITS_G)
        U0 = (0, UNITS_G[0], UNITS_G[0] + UNITS_G[1] + UNITS_A)
        NORMS = (1, 2, 1)
        N0 = (0, NIG, 3 * NIG)
        N_B = 4 * NIG

        block2 = ctx.enter_context(nc.Block())

        @block2.sync
        def _(sp):
            with nc.sync.Fori(0, B) as b:
                sp.wait_ge(s_out, 16 * b + 16)
                sp.nop(nofuse=True)
                sp.dma_start(xs[:, :, :], x1_dram.rearrange("(b t p) c -> b p t c", b=B, p=P)[bass.ds(b, 1)].rearrange("o p t c -> (o p) t c")).then_inc(s_xl, 16)
                sp.wait_ge(s_used, b * UNITS + RING)
                sp.nop(nofuse=True)
                sp.dma_start(at[:, :, :, :].rearrange("p t j n -> p t (j n)"), at_dram.rearrange("(b t p) n -> b p t n", b=B, p=P)[bass.ds(b, 1)].rearrange("o p t n -> (o p) t n")).then_inc(s_atl, 16)
                for l in range(3):
                    H = heads[l]
                    for g in range(NIG):
                        sp.wait_ge(s_row_sb, b * 3 * NIG + l * NIG + g + 1)
                        sp.nop(nofuse=True)
                        sp.dma_start(s_dram[bass.ds(b * (3 * H2) + l * H2, H), g * IG:(g + 1) * IG],
                                     row_sb[g % 2][HPAD:HPAD + H, :]).then_inc(s_row_out[g % 2], 16)
                    for i in range(2):
                        sp.wait_ge(s_row_out[i], 16 * (b * (3 * NIG // 2) + (l + 1) * NIG // 2) + 16)
                        sp.nop(nofuse=True)
                    if H == 1:
                        sp.wait_ge(s_s1_used[0], b * (2 + NIG) + (0 if l == 0 else 1 + NIG) + 1)
                        sp.nop(nofuse=True)
                        sp.dma_start(s1b[0][:, :, :].rearrange("p k n -> p (k n)"),
                                     s_dram[bass.ds(b * (3 * H2) + l * H2, 1), :].to_broadcast([P, N])).then_inc(s_s1[0], 16)
                    else:
                        with nc.sync.Fori(0, NIG) as g:
                            for hh in range(2):
                                sp.wait_ge(s_s1_used[hh], b * (2 + NIG) + g + 2 if hh == 0 else b * NIG + g + 1)
                                sp.nop(nofuse=True)
                                src = s_dram[bass.ds(b * (3 * H2) + l * H2 + hh * 4, 4), bass.ds(g * IG, IG)]
                                sp.dma_start(s1b[hh][:, :, :], src.partition_broadcast(P)).then_inc(s_s1[hh], 16)
                sp.wait_ge(s_x, b * 3 * NIG + 3 * NIG)
                sp.nop(nofuse=True)
                sp.dma_start(out.rearrange("b (t p) c -> b p t c", p=P)[bass.ds(b, 1)].rearrange("o p t c -> (o p) t c"), xs[:, :, :]).then_inc(s_out, 16)
            sp.wait_ge(s_out, 16 * (B + 1))

        @block2.gpsimd
        def _(pool):
            with nc.gpsimd.Fori(0, B * N_B) as n:
                pool.wait_ge(s_var, n + 1)
                pool.nop(nofuse=True)
                nc.gpsimd.tensor_tensor(rs[:, :], mv[:, :, 1], minus_half[:, :], ALU.pow).then_inc(s_rs, 1)

        @block2.scalar
        def _(act):
            a = nc.scalar
            act.sem_inc(s_row_out[0], 16)
            act.sem_inc(s_row_out[1], 16)
            act.sem_inc(s_out, 16)
            with nc.scalar.Fori(0, B) as b:
                for l in range(3):
                    H = heads[l]
                    bl = b * 3 + l
                    for g in range(NIG):
                        for c in range(NC):
                            if g >= 2:
                                act.wait_ge(s_h_ps, bl * NT + (g - 1) * TPG)
                                act.nop(nofuse=True)
                            act.wait_ge(s_xT_ps, bl * (NC * NIG) + g * NC + c + 1)
                            act.nop(nofuse=True)
                            a.copy(xTc[g % 2][:, c, :], xt_ps[c][:, :]).then_inc(s_xT, 1)
                        act.wait_ge(s_row_ps, bl * NIG + g + 1)
                        act.nop(nofuse=True)
                        act.wait_ge(s_row_out[g % 2], 16 * (bl * (NIG // 2) + g // 2 + 1))
                        act.nop(nofuse=True)
                        src, dst = acc[g][HPAD:HPAD + H, :], row_sb[g % 2][HPAD:HPAD + H, :]
                        if l == 1:
                            a.activation(dst, src, ACT.Identity, bias=emb_col[HPAD:HPAD + H, :]).then_inc(s_row_sb, 1)
                        else:
                            a.copy(dst, src).then_inc(s_row_sb, 1)
                        for k in range(TPG):
                            t = g * TPG + k
                            act.wait_ge(s_h_ps, bl * NT + t + 1)
                            act.nop(nofuse=True)
                            if H == 1:
                                a.copy(h_ext[:, t, 0:C], pj_ps[t % 2][:, 0:C])
                            else:
                                a.copy(h_ext[:, t, :].rearrange("p (h w) -> p h w", w=HW)[:, :, 0:HD],
                                       pj_ps[t % 2][:, 0:C].rearrange("p (h d) -> p h d", d=HD))
                            a.copy(sc[:, t, 0:2 * H], pj_ps[t % 2][:, C:C + 2 * H]).then_inc(s_h, 1)
                    act.wait_ge(s_cols, bl + 1)
                    act.nop(nofuse=True)
                    a.activation(v_pos[:, :, 0:H], dd[:, :, 0:H], ACT.Exp, bias=pos_bias[:, :])
                    a.activation(v_neg[:, :, 0:H], dd[:, :, 0:H], ACT.Exp, bias=neg_bias[:, :], scale=NEG_SLOPE)
                    a.activation(f_pos[:, :, 0:H], zz[:, :, 0:H], ACT.Exp)
                    a.activation(f_neg[:, :, 0:H], zp[:, :, 0:H], ACT.Exp, bias=row_bias[:, :], scale=-1.0).then_inc(s_w, 1)
                    for t in range(NT):
                        act.wait_ge(s_vv, bl * NT + t + 1)
                        act.nop(nofuse=True)
                        w = 2 * FW if H == 1 else VW
                        a.copy(vp[:, t, 0, 0:w], vv[t % 2][:, 0:w]).then_inc(s_hi, 1)
                    if l == 1:
                        with nc.scalar.Fori(0, NIG) as g:
                            u = b * UNITS + U0[1] + g * (NT * (1 + H2))
                            ac = b * ACC_B + ACC0[1] + g * (3 * TPG)
                            for j in range(NT):
                                act.wait_ge(s_used, u + j + 1)
                                act.nop(nofuse=True)
                                a.copy(ring[j % RING][:, :].rearrange("p (k n) -> p k n", n=P),
                                       at[:, bass.ds(g * TPG, TPG), j, :]).then_inc(s_amask, 1)
                            act.wait_ge(s_gw, b * NIG + g + 1)
                            act.nop(nofuse=True)
                            for k in range(TPG):
                                act.wait_ge(s_acc, ac + k + 1)
                                act.nop(nofuse=True)
                                a.copy(avs[:, k, :], acc[k][:, 0:H2 * HW]).then_inc(s_free, 1)
                            for hh in range(2):
                                for k in range(TPG):
                                    act.wait_ge(s_acc, ac + (hh + 1) * TPG + k + 1)
                                    act.nop(nofuse=True)
                                    a.copy(gsb[:, k, hh * 4 * 2 * HW:(hh + 1) * 4 * 2 * HW], acc[k][:, 0:4 * 2 * HW]).then_inc(s_free, 1)
                            act.wait_ge(s_min, b * 2 * NIG + g + 1)
                            act.nop(nofuse=True)
                            a.activation(ex[:, :, :], ee[:, :, :], ACT.Exp).then_inc(s_exp, 1)
                    else:
                        with nc.scalar.Fori(0, NIG) as g:
                            ac = b * ACC_B + ACC0[l] + g * (2 * TPG)
                            for k in range(TPG):
                                act.wait_ge(s_acc, ac + k + 1)
                                act.nop(nofuse=True)
                                a.activation(gsb[:, k, 0:FW], acc[k][:, 0:FW], ACT.Copy, scale=f_pos[:, bass.ds(g * TPG + k, 1), 0]).then_inc(s_free, 1)
                            if l == 2:
                                act.wait_ge(s_min, b * 2 * NIG + NIG + g + 1)
                                act.nop(nofuse=True)
                                a.activation(ex[:, :, :], ee[:, :, :], ACT.Exp).then_inc(s_exp, 1)

        @block2.tensor
        def _(pe):
            pe.sem_inc(s_used, RING)
            m = nc.tensor
            with nc.tensor.Fori(0, B) as b:
                for l in range(3):
                    H = heads[l]
                    bl = b * 3 + l
                    for g in range(NIG):
                        if l == 0:
                            pe.wait_ge(s_xl, 16 * b + 16)
                            pe.nop(nofuse=True)
                        else:
                            pe.wait_ge(s_x, bl * NIG)
                            pe.nop(nofuse=True)
                        for c in range(NC):
                            if g > 0:
                                pe.wait_ge(s_xT, bl * (NC * NIG) + (g - 1) * NC + c + 1)
                                pe.nop(nofuse=True)
                            for k in range(TPG):
                                mm = m.transpose(xt_ps[c][:, k * P:(k + 1) * P], xs[:, g * TPG + k, c * P:(c + 1) * P], ident[:, :])
                            mm.then_inc(s_xT_ps, 1)
                        pe.wait_ge(s_xT, bl * (NC * NIG) + (g + 1) * NC)
                        pe.nop(nofuse=True)
                        for c in range(NC):
                            mm = m.matmul(acc[g][0:HPAD + H, :], w_row[l][:, c, :], xTc[g % 2][:, c, :], start=(c == 0), stop=(c == NC - 1))
                        mm.then_inc(s_row_ps, 1)
                        for k in range(TPG):
                            t = g * TPG + k
                            if t >= 2:
                                pe.wait_ge(s_h, bl * NT + t - 1)
                                pe.nop(nofuse=True)
                            for c in range(NC):
                                mm = m.matmul(pj_ps[t % 2][:, 0:C + 2 * H], xTc[g % 2][:, c, k * P:(k + 1) * P], w_ext[l][:, c, :],
                                              start=(c == 0), stop=(c == NC - 1))
                            mm.then_inc(s_h_ps, 1)
                    pe.wait_ge(s_mx, bl + 1)
                    pe.nop(nofuse=True)
                    m.matmul(xt_ps[0][:, 0:H], mxb[0:H, :], ident[0:H, 0:H], start=True, stop=True).then_inc(s_mx_ps, 1)
                    pe.wait_ge(s_hi, bl * NT + NT)
                    pe.nop(nofuse=True)
                    pe.wait_ge(s_lo, bl * NT + NT)
                    pe.nop(nofuse=True)

                    def unit(bank_cols, slot, j, rhs, first, last):
                        for k in range(TPG):
                            for part in range(2):
                                mm = m.matmul(acc[k][:, bank_cols[0]:bank_cols[1]], ring[slot][:, k * P:(k + 1) * P], rhs(part),
                                              start=(first and part == 0), stop=(j == NT - 1 and part == 1),
                                              skip_group_check=True)
                            if last and k < TPG - 1:
                                mm.then_inc(s_acc, 1)
                        return mm

                    if l == 1:
                        with nc.tensor.Fori(0, NIG) as g:
                            am = b * UNITS_A + g * NT
                            gm = b * G_B + G0[1] + g * (NT * H2)
                            fr = b * ACC_B + ACC0[1] + g * (3 * TPG)
                            for j in range(NT):
                                pe.wait_ge(s_amask, am + j + 1)
                                pe.nop(nofuse=True)
                                if j == 0:
                                    pe.wait_ge(s_free, fr + 1)
                                    pe.nop(nofuse=True)
                                mm = unit((0, H2 * HW), j % RING, j,
                                          lambda part: vp[:, j, part, :].rearrange("p (h s w) -> p h s w", s=2, w=HW)[:, :, 1, :],
                                          j == 0, j == NT - 1)
                                mm.then_inc(s_used, 1)
                            pe.drain().then_inc(s_acc, 1)
                            for hh in range(2):
                                pe.wait_ge(s_free, fr + (hh + 1) * TPG + 1)
                                pe.nop(nofuse=True)
                                for j in range(NT):
                                    for h in range(4):
                                        n = (hh * NT + j) * 4 + h
                                        pe.wait_ge(s_mask, gm + n + 1)
                                        pe.nop(nofuse=True)
                                        hd = hh * 4 + h
                                        mm = unit((h * 2 * HW, (h + 1) * 2 * HW), n % RING, j,
                                                  lambda part: vp[:, j, part, hd * 2 * HW:(hd + 1) * 2 * HW],
                                                  j == 0 and h == 0, j == NT - 1 and h == 3)
                                        mm.then_inc(s_used, 1)
                                pe.drain().then_inc(s_acc, 1)
                    else:
                        with nc.tensor.Fori(0, NIG) as g:
                            gm = b * G_B + G0[l] + g * (2 * NT)
                            fr = b * ACC_B + ACC0[l] + g * (2 * TPG)
                            for br in range(2):
                                pe.wait_ge(s_free, fr + br * TPG + 1)
                                pe.nop(nofuse=True)
                                for j in range(NT):
                                    n = br * NT + j
                                    pe.wait_ge(s_mask, gm + n + 1)
                                    pe.nop(nofuse=True)
                                    mm = unit((0, FW), n % RING, j,
                                              lambda part: vp[:, j, part, br * FW:(br + 1) * FW], j == 0, j == NT - 1)
                                    mm.then_inc(s_used, 1)
                                pe.drain().then_inc(s_acc, 1)

        @block2.vector
        def _(dve):
            v = nc.vector
            dve.sem_inc(s_free, 1)
            dve.sem_inc(s_gw, 1)
            dve.sem_inc(s_s1_used[0], 1)
            dve.sem_inc(s_s1_used[1], 1)

            def normalise(dst, src, nth):
                for k in range(TPG):
                    v.bn_stats(st[:, k, :], src[:, k, :])
                dve.drain()
                for k in range(TPG):
                    v.bn_aggr(mv[:, k, :], st[:, k, :])
                dve.drain()
                v.tensor_scalar(mv[:, :, 1], mv[:, :, 1], LN_EPS, None, ALU.add).then_inc(s_var, 1)
                dve.wait_ge(s_rs, nth)
                dve.nop(nofuse=True)
                for k in range(TPG):
                    mm = v.tensor_scalar(dst(k), src[:, k, :], mv[:, k, 0:1], rs[:, k:k + 1], ALU.subtract, ALU.mult)
                return mm

            def elu_add(x_in, nth):
                v.tensor_scalar(ee[:, :, :], yy[:, :, :], 0.0, None, ALU.min).then_inc(s_min, 1)
                dve.drain()
                v.tensor_tensor(yy[:, :, :], yy[:, :, :], ee[:, :, :], ALU.subtract)
                dve.drain()
                v.tensor_tensor(yy[:, :, :], yy[:, :, :], x_in, ALU.add)
                dve.wait_ge(s_exp, nth)
                dve.nop(nofuse=True)
                dve.drain()
                v.scalar_tensor_tensor(yy[:, :, :], ex[:, :, :], -1.0, yy[:, :, :], ALU.add, ALU.add)
                dve.drain()

            with nc.vector.Fori(0, B) as b:
                for l in range(3):
                    H = heads[l]
                    bl = b * 3 + l
                    for g in range(NIG):
                        dve.wait_ge(s_row_ps, bl * NIG + g + 1)
                        dve.nop(nofuse=True)
                        v.tensor_reduce(mx4[0:H, g:g + 1], acc[g][0:H, :], AX.X, ALU.max)
                    if H == 1:
                        v.memset(h_ext[:, :, C:C + 1], 1.0)
                        v.memset(h_ext[:, :, C + 1:C + 2], 0.0)
                    else:
                        hx = h_ext[:, :, :].rearrange("p t (h w) -> p (t h) w", w=HW)
                        v.memset(hx[:, :, HD:HD + 1], 1.0)
                        v.memset(hx[:, :, HD + 1:HD + 2], 0.0)
                    dve.drain()
                    v.tensor_reduce(mx[0:H, :], mx4[0:H, :], AX.X, ALU.max)
                    dve.drain()
                    v.tensor_copy(mxb[0:H, :], mx[0:H, 0:1].to_broadcast([H, P])).then_inc(s_mx, 1)
                    dve.wait_ge(s_mx_ps, bl + 1)
                    dve.nop(nofuse=True)
                    dve.wait_ge(s_h, bl * NT + NT)
                    dve.nop(nofuse=True)
                    top_bc = xt_ps[0][:, 0:H].unsqueeze(1).to_broadcast([P, NT, H])
                    v.tensor_tensor(dd[:, :, 0:H], sc[:, :, 0:H], top_bc, ALU.subtract)
                    v.tensor_tensor(zz[:, :, 0:H], sc[:, :, H:2 * H], top_bc, ALU.add)
                    v.tensor_scalar(nsd[:, :, 0:H], sc[:, :, 0:H], -1.0, None, ALU.mult)
                    dve.drain()
                    if l == 1:
                        v.tensor_tensor(zz[:, :, :], zz[:, :, :], emb_bc[:, :].unsqueeze(1).to_broadcast([P, NT, H2]), ALU.add)
                        dve.drain()
                    v.tensor_scalar(zp[:, :, 0:H], zz[:, :, 0:H], 1.0 - NEG_SLOPE, 0.0, ALU.mult, ALU.max)
                    dve.drain()
                    v.tensor_scalar(zz[:, :, 0:H], zz[:, :, 0:H], 1.0 - NEG_SLOPE, 0.0, ALU.mult, ALU.min).then_inc(s_cols, 1)
                    dve.wait_ge(s_w, bl + 1)
                    dve.nop(nofuse=True)
                    for t in range(NT + 1):
                        if t < NT:
                            if t >= 2:
                                dve.wait_ge(s_lo, bl * NT + t - 1)
                                dve.nop(nofuse=True)
                            if H == 1:
                                v.tensor_scalar(vv[t % 2][:, 0:FW], h_ext[:, t, 0:FW], v_pos[:, t, 0:1], None, ALU.mult)
                                v.tensor_scalar(vv[t % 2][:, FW:2 * FW], h_ext[:, t, 0:FW], v_neg[:, t, 0:1], None, ALU.mult).then_inc(s_vv, 1)
                            else:
                                he = h_ext[:, t, :].rearrange("p (h w) -> p h w", w=HW)
                                ve = vv[t % 2][:, :].rearrange("p (h s w) -> p h s w", s=2, w=HW)
                                v.tensor_tensor(ve[:, :, 0, :], he, v_pos[:, t, :].unsqueeze(2).to_broadcast([P, H2, HW]), ALU.mult)
                                v.tensor_tensor(ve[:, :, 1, :], he, v_neg[:, t, :].unsqueeze(2).to_broadcast([P, H2, HW]), ALU.mult).then_inc(s_vv, 1)
                        if t > 0:
                            w = 2 * FW if H == 1 else VW
                            dve.wait_ge(s_hi, bl * NT + t)
                            dve.nop(nofuse=True)
                            v.tensor_tensor(vp[:, t - 1, 1, 0:w], vv[(t - 1) % 2][:, 0:w], vp[:, t - 1, 0, 0:w].bitcast(F32), ALU.subtract).then_inc(s_lo, 1)
                    if l == 0:
                        dve.wait_ge(s_atl, 16 * b + 16)
                        dve.nop(nofuse=True)
                    if l == 1:
                        with nc.vector.Fori(0, NIG) as g:
                            u = b * UNITS + U0[1] + g * (NT * (1 + H2)) + NT
                            for hh in range(2):
                                dve.wait_ge(s_s1[hh], 16 * (b * (2 + NIG) + g + 2) if hh == 0 else 16 * (b * NIG + g + 1))
                                dve.nop(nofuse=True)
                                for j in range(NT):
                                    for h in range(4):
                                        n = (hh * NT + j) * 4 + h
                                        dve.wait_ge(s_used, u + n + 1)
                                        dve.nop(nofuse=True)
                                        mm = v.scalar_tensor_tensor(
                                            ring[n % RING][:, :].rearrange("p (k n) -> p k n", n=P),
                                            s1b[hh][:, h, :].rearrange("p (k n) -> p k n", n=P),
                                            nsd[:, j, hh * 4 + h:hh * 4 + h + 1],
                                            at[:, bass.ds(g * TPG, TPG), j, :], ALU.is_gt, ALU.mult).then_inc(s_mask, 1)
                                dve.drain().then_inc(s_s1_used[hh], 1)
                            dve.wait_ge(s_free, b * ACC_B + ACC0[1] + (g + 1) * (3 * TPG) + 1)
                            dve.nop(nofuse=True)
                            gv = gsb[:, :, :].rearrange("p k (h s w) -> p (k h) s w", s=2, w=HW)
                            av = avs[:, :, :].rearrange("p k (h w) -> p (k h) w", w=HW)
                            tv = tot[:, :, :].rearrange("p k (h w) -> p (k h) w", w=HW)
                            def per_row(f):
                                return f[:, bass.ds(g * TPG, TPG), :].rearrange("p k h -> p (k h)").unsqueeze(2).to_broadcast([P, TPG * H2, HW])
                            v.tensor_tensor(av, av, gv[:, :, 1, :], ALU.subtract)
                            v.tensor_tensor(tv, gv[:, :, 0, :], per_row(f_pos), ALU.mult)
                            dve.drain()
                            v.tensor_tensor(av, av, per_row(f_neg), ALU.mult)
                            dve.drain()
                            v.tensor_tensor(tv, tv, av, ALU.add).then_inc(s_gw, 1)
                            dve.drain()
                            v.reciprocal(rden[:, :, :].rearrange("p k h -> p (k h)"), tv[:, :, HD])
                            dve.drain()
                            v.tensor_tensor(yy[:, :, :].rearrange("p k (h d) -> p (k h) d", d=HD), tv[:, :, 0:HD],
                                            rden[:, :, :].rearrange("p k h -> p (k h)").unsqueeze(2).to_broadcast([P, TPG * H2, HD]), ALU.mult)
                            dve.drain()
                            normalise(lambda k: yy[:, k, :], yy, b * N_B + N0[1] + g * 2 + 1)
                            dve.drain()
                            v.tensor_tensor(yy[:, :, :], yy[:, :, :], gamma_bc[:, :].unsqueeze(1).to_broadcast([P, TPG, C]), ALU.mult)
                            dve.drain()
                            v.tensor_tensor(yy[:, :, :], yy[:, :, :], beta_bc[:, :].unsqueeze(1).to_broadcast([P, TPG, C]), ALU.add)
                            dve.drain()
                            elu_add(xs[:, bass.ds(g * TPG, TPG), :], b * 2 * NIG + g + 1)
                            normalise(lambda k: xs[:, bass.ds(g * TPG + k, 1), :].rearrange("p o c -> p (o c)"), yy, b * N_B + N0[1] + g * 2 + 2).then_inc(s_x, 1)
                    else:
                        dve.wait_ge(s_s1[0], 16 * (b * (2 + NIG) + (1 if l == 0 else 2 + NIG)))
                        dve.nop(nofuse=True)
                        with nc.vector.Fori(0, NIG) as g:
                            u = b * UNITS + U0[l] + g * (2 * NT)
                            s1 = s1b[0][:, bass.ds(g, 1), :].rearrange("p o (k n) -> p (o k) n", n=P)
                            for br in range(2):
                                for j in range(NT):
                                    n = br * NT + j
                                    dve.wait_ge(s_used, u + n + 1)
                                    dve.nop(nofuse=True)
                                    v.scalar_tensor_tensor(
                                        ring[n % RING][:, :].rearrange("p (k n) -> p k n", n=P), s1, nsd[:, j, 0:1],
                                        at[:, bass.ds(g * TPG, TPG), j, :], ALU.is_le if br else ALU.is_gt, ALU.mult).then_inc(s_mask, 1)
                            ac = b * ACC_B + ACC0[l] + g * (2 * TPG)
                            dve.wait_ge(s_free, ac + TPG + 1)
                            dve.nop(nofuse=True)
                            for k in range(TPG):
                                dve.wait_ge(s_acc, ac + TPG + k + 1)
                                dve.nop(nofuse=True)
                                v.scalar_tensor_tensor(tot[:, k, 0:FW], acc[k][:, 0:FW], f_neg[:, bass.ds(g * TPG + k, 1), 0],
                                                       gsb[:, k, 0:FW], ALU.mult, ALU.add).then_inc(s_free, 1)
                            dve.drain()
                            v.reciprocal(rden[:, :, 0], tot[:, :, C])
                            dve.drain()
                            xg = xs[:, bass.ds(g * TPG, TPG), :]
                            if l == 0:
                                for k in range(TPG):
                                    v.scalar_tensor_tensor(yy[:, k, :], tot[:, k, 0:C], rden[:, k, 0:1],
                                                           xs[:, bass.ds(g * TPG + k, 1), :].rearrange("p o c -> p (o c)"), ALU.mult, ALU.add)
                            else:
                                for k in range(TPG):
                                    v.tensor_scalar(yy[:, k, :], tot[:, k, 0:C], rden[:, k, 0:1], None, ALU.mult)
                            dve.drain()
                            if l == 2:
                                elu_add(xg, b * 2 * NIG + NIG + g + 1)
                            normalise(lambda k: xs[:, bass.ds(g * TPG + k, 1), :].rearrange("p o c -> p (o c)"), yy, b * N_B + N0[l] + g + 1).then_inc(s_x, 1)
                        dve.drain().then_inc(s_s1_used[0], 1)


_INS = ['x', 'adj', 'L0_gnn_W', 'L0_gnn_b', 'L1_gnn_W', 'L1_gnn_a', 'L2_gnn_W', 'L2_gnn_a1', 'L2_gnn_a2',
        'L2_gnn_edge_emb', 'L2_gnn_ln_gamma', 'L2_gnn_ln_beta', 'L3_gnn_W', 'L3_gnn_a']


def kernel(**inputs):
    import numpy as _np
    import concourse.bacc as _bacc
    from concourse import mybir as _mybir
    from concourse.bass_utils import run_bass_kernel_spmd as _run

    nc = _bacc.Bacc("TRN2", target_bir_lowering=False, num_devices=1)
    arrays, args = {}, []
    for name in _INS:
        a = _np.ascontiguousarray(inputs[name])
        arrays[f"in_{name}_dram"] = a
        args.append(nc.dram_tensor(f"in_{name}_dram", a.shape, _mybir.dt.from_np(a.dtype), kind="ExternalInput").ap())
    shape = inputs['x'].shape
    args.append(nc.dram_tensor("out_dram", shape, _mybir.dt.float32, kind="ExternalOutput").ap())
    four_layer_graph_kernel(nc, *args)
    r = _run(nc, [arrays], core_ids=[0])
    return r.results[0]["out_dram"]
```

```python
from contextlib import ExitStack

import numpy as np

import concourse.bass as bass
from concourse import mybir

F32 = mybir.dt.float32
F32R = mybir.dt.float32r
F16 = mybir.dt.float16
BF16 = mybir.dt.bfloat16
I32 = mybir.dt.int32
U8 = mybir.dt.uint8
ALU = mybir.AluOpType
ACT = mybir.ActivationFunctionType
AX = mybir.AxisListType

P = 128
SLOTS = 25
ROUNDS = 4
LN_EPS = 1e-5
BIG = 3.0e38
POS_SHIFT = 60.0
NEG_SHIFT = 20.0
NEG_SLOPE = 0.2
PARTS = 3
RING = 8
ARING = 4
VSLOTS = 3
IG = 512
SPARE = 2
POWER_AFTER = 4
HPAD = 32


def four_layer_graph_kernel(nc, x, adj, w0, b0, w1, a1, w2, a2s, a2d, emb, gamma, beta, w3, a3, out):
    B, N, C = x.shape
    NT = N // P
    NC = C // P
    HD = a2s.shape[0]
    H2 = C // HD
    NIG = N // IG
    TPG = IG // P
    ROWS = B * NT

    x_rows = x.rearrange("b n c -> (b n) c")
    adj_rows = adj.rearrange("b n m -> (b n) m")
    out_rows = out.rearrange("b n c -> (b n) c")

    with ExitStack() as ctx:
        def sb(name, shape, dt):
            return ctx.enter_context(nc.sbuf_tensor(name, shape, dt))

        def psum(name, shape, dt):
            return ctx.enter_context(nc.psum_tensor(name, shape, dt))

        def sem(name):
            return ctx.enter_context(nc.semaphore(name))

        x1_dram = nc.dram_tensor("x1_scratch", (B * N, C), F32, kind="Internal").ap()
        at_dram = nc.dram_tensor("at_scratch", (B * NT * P, N), U8, kind="Internal").ap()
        s_dram = nc.dram_tensor("s_scratch", (B * 3 * H2, N), F32, kind="Internal").ap()

        ident = sb("ident", [P, P], F32)
        ident_bf = sb("ident_bf", [P, P], BF16)
        countdown = sb("countdown", [P, N], F16)
        w0_sb = sb("w0_sb", [P, 2 * NC, C], F32)
        b0_bc = sb("b0_bc", [P, C], F32)
        w_ext = [sb(f"w_ext{l}", [P, NC, C + 2 * h], F32) for l, h in ((1, 1), (2, H2), (3, 1))]
        emb_bc = sb("emb_bc", [P, H2], F32)
        emb_col = sb("emb_col", [HPAD + H2, 1], F32)
        gamma_bc = sb("gamma_bc", [P, C], F32)
        beta_bc = sb("beta_bc", [P, C], F32)
        pos_bias = sb("pos_bias", [P, 1], F32)
        neg_bias = sb("neg_bias", [P, 1], F32)
        row_bias = sb("row_bias", [P, 1], F32)
        graph_row = sb("graph_row", [P, ROWS], F32)
        minus_half = sb("minus_half", [P, TPG], F32)

        ps = [psum(f"ps{i}", [P, 512], F32) for i in range(8)]
        acc = ps[0:4]
        xt_ps = ps[4:6]
        pj_ps = ps[6:8]
        at_ps = [ps[i][:, :].bitcast(BF16) for i in (0, 1)]

        with ExitStack() as tmp:
            def tsb(name, shape, dt):
                return tmp.enter_context(nc.sbuf_tensor(name, shape, dt))
            a_bc = {k: tsb(f"abc_{k}", [P, n], F32) for k, n in (("1s", C), ("1d", C), ("2s", HD), ("2d", HD), ("3s", C), ("3d", C))}
            w3_in = tsb("w3_in", [P, NC, C], F32)
            prod = tsb("prod", [P, NC, C], F32)
            s_load = tmp.enter_context(nc.semaphore("s_load"))
            s_id = tmp.enter_context(nc.semaphore("s_id"))
            s_w3 = tmp.enter_context(nc.semaphore("s_w3"))
            s_step = tmp.enter_context(nc.semaphore("s_step"))
            loads = [
                (w0_sb[:, :, :], w0.rearrange("(k p) n -> p k n", p=P)),
                (w_ext[0][:, :, 0:C], w1.rearrange("(k p) n -> p k n", p=P)),
                (w_ext[1][:, :, 0:C], w2.rearrange("(k p) n -> p k n", p=P)),
                (w3_in[:, :, :], w3.rearrange("(k p) n -> p k n", p=P)),
                (b0_bc[:, :], b0.partition_broadcast(P)),
                (gamma_bc[:, :], gamma.partition_broadcast(P)),
                (beta_bc[:, :], beta.partition_broadcast(P)),
                (a_bc["1s"][:, :], a1[0:C].partition_broadcast(P)),
                (a_bc["1d"][:, :], a1[C:2 * C].partition_broadcast(P)),
                (a_bc["2s"][:, :], a2s.partition_broadcast(P)),
                (a_bc["2d"][:, :], a2d.partition_broadcast(P)),
                (a_bc["3s"][:, :], a3[0, 0:C].partition_broadcast(P)),
                (a_bc["3d"][:, :], a3[0, C:2 * C].partition_broadcast(P)),
                (emb_bc[:, :], emb[1, :].partition_broadcast(P)),
                (emb_col[HPAD:HPAD + H2, :], emb[1:2, :].rearrange("o h -> h o")),
            ]
            with nc.Block() as block0:
                @block0.sync
                def _(sp):
                    with nc.allow_non_contiguous_dma(reason="eight numbers, one to a partition"):
                        for dst, src in loads:
                            sp.dma_start(dst, src).then_inc(s_load, 16)

                @block0.gpsimd
                def _(pool):
                    nc.gpsimd.iota(countdown[:, :], pattern=[[-1, N]], base=N, channel_multiplier=0,
                                   allow_small_or_imprecise_dtypes=True)
                    nc.gpsimd.iota(graph_row[:, :].rearrange("p (b t) -> p b t", b=B), pattern=[[N, B], [0, NT]], base=0,
                                   channel_multiplier=0, allow_small_or_imprecise_dtypes=True)
                    nc.gpsimd.memset(minus_half[:, :], -0.5)
                    nc.gpsimd.memset(pos_bias[:, :], POS_SHIFT)
                    nc.gpsimd.memset(neg_bias[:, :], -NEG_SHIFT)
                    nc.gpsimd.memset(row_bias[:, :], POS_SHIFT + NEG_SHIFT)
                    nc.gpsimd.memset(ident[:, :], 0.0).then_inc(s_id, 1)
                    pool.wait_ge(s_id, 1)
                    nc.gpsimd.affine_select(out=ident[:, :], in_=ident[:, :], compare_op=ALU.not_equal, fill=1.0,
                                            base=0, pattern=[[-1, P]], channel_multiplier=1).then_inc(s_id, 1)
                    pool.wait_ge(s_id, 2)
                    nc.gpsimd.tensor_copy(ident_bf[:, :], ident[:, :])

                @block0.tensor
                def _(pe):
                    pe.wait_ge(s_id, 2)
                    pe.wait_ge(s_load, 16 * len(loads))
                    for k in range(NC):
                        for o in range(NC):
                            mm = nc.tensor.transpose(ps[k][:, o * P:(o + 1) * P], w3_in[:, o, k * P:(k + 1) * P], ident[:, :])
                    mm.then_inc(s_w3, 1)

                @block0.vector
                def _(dve):
                    v = nc.vector
                    dve.wait_ge(s_load, 16 * len(loads))
                    dve.wait_ge(s_w3, 1)
                    for k in range(NC):
                        v.tensor_copy(w_ext[2][:, k, 0:C], ps[k][:, 0:C])
                    dve.drain()
                    for l, H, ends in ((0, 1, ("1d", "1s")), (1, H2, ("2d", "2s")), (2, 1, ("3d", "3s"))):
                        for e, end in enumerate(ends):
                            for k in range(NC):
                                pv = prod[:, k, :].rearrange("p (h d) -> p h d", h=H)
                                v.tensor_tensor(pv, w_ext[l][:, k, 0:C].rearrange("p (h d) -> p h d", h=H),
                                                a_bc[end][:, :].unsqueeze(1).to_broadcast([P, H, C // H]), ALU.mult)
                            dve.drain()
                            for k in range(NC):
                                pv = prod[:, k, :].rearrange("p (h d) -> p h d", h=H)
                                v.tensor_reduce(w_ext[l][:, k, C + e * H:C + (e + 1) * H], pv, AX.X, ALU.add)
                            dve.drain()

        stage_a = ctx.enter_context(ExitStack())
        def sb(name, shape, dt):
            return stage_a.enter_context(nc.sbuf_tensor(name, shape, dt))

        a_int = sb("a_int", [P, N], I32)
        a_bf = [sb(f"a_bf{i}", [P, N], BF16) for i in range(2)]
        prio = sb("prio", [P, N], F16)
        top = sb("top", [P, 8 * ROUNDS], F32)
        pad = sb("pad", [P, 8 * ROUNDS], F32)
        idx = [sb(f"idx{i}", [P, 8 * ROUNDS], I32) for i in range(2)]
        clamp = [sb(f"clamp{i}", [P, 2], F32) for i in range(2)]
        nbr = [sb(f"nbr{i}", [P, SLOTS, C], F32) for i in range(2)]
        at_stage = sb("at_stage", [P, N], U8)
        x_in = [sb(f"x_in{i}", [P, C], F32) for i in range(2)]
        agg = sb("agg", [P, C], F32)
        hT = sb("hT", [P, 2 * NC, P], F32)
        y0 = sb("y0", [P, C], F32)
        st0 = sb("st0", [P, 6], F32)
        mv0 = sb("mv0", [P, 2], F32)
        rs0 = sb("rs0", [P, 1], F32)

        block = stage_a.enter_context(nc.Block())

        s_adj = sem("s_adj")
        s_xin = [sem(f"s_xin{i}") for i in range(2)]
        s_int_used = sem("s_int_used")
        s_bf_dve = sem("s_bf_dve")
        s_bf_pe = sem("s_bf_pe")
        s_bf_used = sem("s_bf_used")
        s_at_ps = sem("s_at_ps")
        s_at_ps_used = sem("s_at_ps_used")
        s_at_sb = sem("s_at_sb")
        s_at_out = sem("s_at_out")
        s_idx = sem("s_idx")
        s_gath = [sem(f"s_gath{i}") for i in range(2)]
        s_red = sem("s_red")
        s_agg = sem("s_agg")
        s_hT_ps = sem("s_hT_ps")
        s_hT = sem("s_hT")
        s_y0 = sem("s_y0")
        s_var0 = sem("s_var0")
        s_rs0 = sem("s_rs0")
        s_x1 = sem("s_x1")
        s_x1_out = sem("s_x1_out")

        def steps(engine, step, first=1, stop=ROWS - 1):
            with engine.Fori(0, (stop - first) // 2) as u:
                for half in range(2):
                    step(u * 2 + (first + half), (first + half) % 2, u + (first + half) // 2 + 1)

        @block.sync
        def _(sp):
            def load_adj(t):
                sp.wait_ge(s_int_used, 1)
                sp.sem_inc(s_int_used, -1)
                sp.dma_start(a_int[:, :], adj_rows[bass.ds(t * P, P), :]).then_inc(s_adj, 16)

            def store_at(t):
                sp.wait_ge(s_at_sb, 1)
                sp.sem_inc(s_at_sb, -1)
                sp.dma_start(at_dram[bass.ds(t * P, P), :], at_stage[:, :]).then_inc(s_at_out, 16)

            def load_x(t, par):
                sp.dma_start(x_in[par][:, :], x_rows[bass.ds(t * P, P), :]).then_inc(s_xin[par], 16)

            def store_x1(t):
                sp.wait_ge(s_x1, 1)
                sp.sem_inc(s_x1, -1)
                sp.dma_start(x1_dram[bass.ds(t * P, P), :], y0[:, :]).then_inc(s_x1_out, 16)

            def step(t, par, nth=None, lead=True):
                if lead:
                    load_adj(t + 2)
                store_at(t + 1)
                store_x1(t + (-1))
                load_x(t + 1, 1 - par)

            load_adj(0)
            load_adj(1)
            for t in (-1, 0):
                if t == 0:
                    load_adj(2)
                store_at(t + 1)
                load_x(t + 1, (t + 1) % 2)
            steps(nc.sync, step, 1, ROWS - 3)
            step(ROWS - 3, (ROWS - 3) % 2)
            step(ROWS - 2, ROWS % 2, lead=False)
            store_x1(ROWS - 2)
            store_x1(ROWS - 1)
            sp.wait_ge(s_at_out, 16)
            sp.wait_ge(s_x1_out, 16)

        @block.gpsimd
        def _(pool):
            def power():
                pool.wait_ge(s_var0, 1)
                pool.sem_inc(s_var0, -1)
                nc.gpsimd.tensor_tensor(rs0[:, :], mv0[:, 1:2], minus_half[:, 0:1], ALU.pow).then_inc(s_rs0, 1)

            def gathers(par, with_power=True):
                pool.wait_ge(s_idx, 1)
                pool.sem_inc(s_idx, -1)
                pool.wait_ge(s_red, 1)
                pool.sem_inc(s_red, -1)
                for k in range(SLOTS):
                    nc.gpsimd.indirect_dma_start(
                        out=nbr[par][:, k, :], out_offset=None, in_=x_rows,
                        in_offset=bass.IndirectOffsetOnAxis(ap=idx[par][:, k:k + 1], axis=0)).then_inc(s_gath[par], 16)
                    if k == POWER_AFTER and with_power:
                        power()

            gathers(0, with_power=False)
            gathers(1, with_power=False)
            steps(nc.gpsimd, lambda t, par, nth: gathers(1 - par))
            power()
            power()

        @block.scalar
        def _(act):
            act.sem_inc(s_int_used, 1)
            act.sem_inc(s_at_out, 16)
            act.sem_inc(s_at_ps_used, 2)

            def to_bf16(par):
                act.wait_ge(s_adj, 16)
                act.sem_inc(s_adj, -16)
                act.wait_ge(s_bf_used, 1)
                act.sem_inc(s_bf_used, -1)
                nc.scalar.copy(a_bf[par][:, :], a_int[:, :]).then_inc(s_bf_dve, 1)
                act.drain().then_inc(s_bf_pe, 1)
                act.drain().then_inc(s_int_used, 1)

            def copy_at():
                act.wait_ge(s_at_out, 16)
                act.sem_inc(s_at_out, -16)
                for q in range(2):
                    act.wait_ge(s_at_ps, 1)
                    act.sem_inc(s_at_ps, -1)
                    nc.scalar.copy(at_stage[:, q * (N // 2):(q + 1) * (N // 2)], at_ps[q][:, 0:N // 2]).then_inc(s_at_ps_used, 1)
                act.drain().then_inc(s_at_sb, 1)

            def copy_hT():
                act.wait_ge(s_hT_ps, 1)
                act.sem_inc(s_hT_ps, -1)
                nc.scalar.copy(hT[:, :, :].rearrange("p k n -> p (k n)"), xt_ps[0][:, :]).then_inc(s_hT, 1)

            def step(t, par, nth=None, lead=True):
                copy_at()
                if lead:
                    to_bf16(par)
                copy_hT()

            to_bf16(0)
            to_bf16(1)
            copy_at()
            step(0, 0)
            steps(nc.scalar, step, 1, ROWS - 3)
            step(ROWS - 3, 1)
            step(ROWS - 2, 0, lead=False)
            copy_hT()

        @block.tensor
        def _(pe):
            def transpose_adj(par):
                pe.wait_ge(s_bf_pe, 1)
                pe.sem_inc(s_bf_pe, -1)
                for q in range(2):
                    pe.wait_ge(s_at_ps_used, 1)
                    pe.sem_inc(s_at_ps_used, -1)
                    for k in range(NT // 2):
                        j = q * (NT // 2) + k
                        mm = nc.tensor.transpose(at_ps[q][:, k * P:(k + 1) * P], a_bf[par][:, j * P:(j + 1) * P], ident_bf[:, :])
                    mm.then_inc(s_at_ps, 1)

            def products(par):
                pe.wait_ge(s_xin[par], 16)
                pe.sem_inc(s_xin[par], -16)
                pe.wait_ge(s_agg, 1)
                pe.sem_inc(s_agg, -1)
                for k in range(2 * NC):
                    src = x_in[par] if k < NC else agg
                    c = k % NC
                    mm = nc.tensor.transpose(xt_ps[0][:, k * P:(k + 1) * P], src[:, c * P:(c + 1) * P], ident[:, :])
                mm.then_inc(s_hT_ps, 1)
                pe.wait_ge(s_hT, 1)
                pe.sem_inc(s_hT, -1)
                for k in range(2 * NC):
                    mm = nc.tensor.matmul(pj_ps[0][:, 0:C], hT[:, k, :], w0_sb[:, k, :],
                                          start=(k == 0), stop=(k == 2 * NC - 1))
                mm.then_inc(s_y0, 1)

            def step(t, par, nth=None):
                transpose_adj(1 - par)
                products(par)

            transpose_adj(0)
            step(0, 0)
            steps(nc.tensor, step)
            products(1)

        @block.vector
        def _(dve):
            v = nc.vector
            dve.sem_inc(s_bf_used, 2)
            dve.sem_inc(s_red, 2)
            dve.sem_inc(s_x1_out, 16)

            def choose(t, par):
                dve.wait_ge(s_bf_dve, 1)
                dve.sem_inc(s_bf_dve, -1)
                v.tensor_tensor(prio[:, :], a_bf[par][:, :], countdown[:, :], ALU.mult).then_inc(s_bf_used, 1)
                dve.drain()
                for r in range(ROUNDS):
                    v.max(top[:, 8 * r:8 * r + 8], prio[:, :])
                    dve.drain()
                    if r < ROUNDS - 1:
                        v.match_replace(prio[:, :], top[:, 8 * r:8 * r + 8], prio[:, :], 0.0)
                        dve.drain()
                v.tensor_scalar(clamp[par][:, 0:1], top[:, 0:1], 0.0, BIG, ALU.is_gt, ALU.mult)
                v.tensor_scalar(clamp[par][:, 1:2], top[:, SLOTS:SLOTS + 1], 0.0, -BIG, ALU.is_gt, ALU.mult)
                v.tensor_scalar(pad[:, :], top[:, :], 0.0, top[:, 0:1], ALU.is_equal, ALU.mult)
                dve.drain()
                v.tensor_tensor(pad[:, :], pad[:, :], top[:, :], ALU.add)
                dve.drain()
                v.tensor_scalar(pad[:, :], pad[:, :], -1.0, float(N), ALU.mult, ALU.add)
                dve.drain()
                v.tensor_scalar(idx[par][:, :], pad[:, :], float(N - 1), graph_row[:, bass.ds(t, 1)], ALU.min, ALU.add).then_inc(s_idx, 1)

            def maximum(par, nth):
                dve.wait_ge(s_gath[par], nth * (16 * SLOTS))
                dve.nop(nofuse=True)
                v.tensor_reduce(agg[:, :], nbr[par][:, :, :].rearrange("p s c -> p c s"), AX.X, ALU.max).then_inc(s_red, 1)
                dve.drain()
                v.tensor_scalar(agg[:, :], agg[:, :], clamp[par][:, 0:1], clamp[par][:, 1:2], ALU.min, ALU.max).then_inc(s_agg, 1)

            def residual(par):
                dve.wait_ge(s_y0, 1)
                dve.sem_inc(s_y0, -1)
                dve.wait_ge(s_x1_out, 16)
                dve.sem_inc(s_x1_out, -16)
                v.tensor_tensor(y0[:, :], pj_ps[0][:, 0:C], b0_bc[:, :], ALU.add)
                dve.drain()
                v.scalar_tensor_tensor(y0[:, :], y0[:, :], 0.0, x_in[par][:, :], ALU.max, ALU.add)
                dve.drain()
                v.bn_stats(st0[:, :], y0[:, :])
                dve.drain()
                v.bn_aggr(mv0[:, :], st0[:, :])
                dve.drain()
                v.tensor_scalar(mv0[:, 1:2], mv0[:, 1:2], LN_EPS, None, ALU.add).then_inc(s_var0, 1)

            def scale_rows():
                dve.wait_ge(s_rs0, 1)
                dve.sem_inc(s_rs0, -1)
                v.tensor_scalar(y0[:, :], y0[:, :], mv0[:, 0:1], rs0[:, 0:1], ALU.subtract, ALU.mult).then_inc(s_x1, 1)
                dve.drain()

            def step(t, par, nth, lead=True):
                if lead:
                    choose(t + 1, 1 - par)
                residual(1 - par)
                maximum(par, nth)
                scale_rows()

            choose(0, 0)
            choose(1, 1)
            maximum(0, 1)
            steps(nc.vector, step)
            step(ROWS - 1, 1, ROWS // 2, lead=False)
            residual(1)
            scale_rows()


        stage_a.close()

        def sb(name, shape, dt):
            return ctx.enter_context(nc.sbuf_tensor(name, shape, dt))

        HW = HD + 2
        FW = C + 2
        VW = 2 * H2 * HW
        heads = (1, H2, 1)
        HEAD_GROUPS = ((0, 3), (3, H2))
        G_SPLIT = HEAD_GROUPS[0][1] * 2 * HW

        def shared(name, groups):
            def nbytes(shape, dt):
                return int(np.prod(shape[1:])) * (2 if dt is BF16 else 4)
            groups = [[(n, shape, dt[0] if dt else F32) for n, shape, *dt in g] for g in groups]
            size = max(sum(nbytes(shape, dt) for _, shape, dt in g) for g in groups)
            size = -(-size // 32) * 32
            base = -(-nc.sbuf_base // 32) * 32
            sb(name, [P, size // 4], F32)
            placed = []
            for g in groups:
                at_byte = base
                for n, shape, dt in g:
                    placed.append(nc.alloc_sbuf_tensor_at(n, shape, dt, offset=at_byte))
                    at_byte += nbytes(shape, dt)
            return placed

        h_ext, tot, yy, ee, ex = shared("region_h", (
            [("h_ext", [P, NT, H2 * HW])],
            [("tot", [P, TPG, H2 * HW]), ("yy", [P, TPG, C]), ("ee", [P, TPG, C]), ("ex", [P, TPG, C])]))
        *xTc, gsb = shared("region_x", (
            [("xTc0", [P, NC, IG]), ("xTc1", [P, NC, IG])],
            [("gsb", [P, TPG, VW])]))
        *vv, avs = shared("region_v", (
            [(f"vv{i}", [P, VW]) for i in range(VSLOTS)],
            [("avs", [P, TPG, H2 * HW])]))
        xs = sb("xs", [P, NT, C], F32)
        at = sb("at", [P, NT, NT, P], U8)
        vp, vb = shared("region_w", (
            [("vp", [P, NT, 2, 2 * FW], F32R)],
            [("vb", [P, NT, PARTS, VW], BF16)]))
        sc = sb("sc", [P, NT, HPAD + H2], F32)
        row_sb = [sb(f"row_sb{i}", [HPAD + H2, IG], F32) for i in range(2)]
        s1b = [sb(f"s1b{i}", [P, n, IG], F32) for i, n in enumerate((NIG, H2 - HEAD_GROUPS[0][1]))]
        masks = shared("region_m", (
            [(f"ring{i}", [P, IG], F32R) for i in range(RING)],
            [(f"ringb{i}", [P, IG], BF16) for i in range(RING)] + [(f"aring{i}", [P, IG], BF16) for i in range(ARING)]))
        ring, ringb, aring = masks[:RING], masks[RING:2 * RING], masks[2 * RING:]
        mx4 = sb("mx4", [H2, NIG], F32)
        mx = sb("mx", [H2, 1], F32)
        mxb = vv[0][0:H2, 0:P]
        zp = vv[1][:, 0:NT * H2].rearrange("p (t h) -> p t h", h=H2)
        dd = sb("dd", [P, NT, H2], F32)
        nsd = sb("nsd", [P, NT, H2], F32)
        zz = sb("zz", [P, NT, H2], F32)
        v_pos = sb("v_pos", [P, NT, H2], F32)
        v_neg = sb("v_neg", [P, NT, H2], F32)
        f_pos = sb("f_pos", [P, NT, H2], F32)
        f_neg = sb("f_neg", [P, NT, H2], F32)
        rden = sb("rden", [P, TPG, H2], F32)
        st = sb("st", [P, TPG, 6], F32)
        mv = sb("mv", [P, TPG, 2], F32)
        rs = sb("rs", [P, TPG], F32)

        s_xl = [sem(f"s_xl{g}") for g in range(NIG)]
        s_atl = sem("s_atl")
        s_xT_ps = sem("s_xT_ps")
        s_xT = sem("s_xT")
        s_row_ps = sem("s_row_ps")
        s_row_sb = sem("s_row_sb")
        s_row_out = [sem(f"s_row_out{i}") for i in range(2)]
        s_h_ps = sem("s_h_ps")
        s_h = sem("s_h")
        s_mx = sem("s_mx")
        s_mx_ps = sem("s_mx_ps")
        s_cols = sem("s_cols")
        s_w = sem("s_w")
        s_vv = sem("s_vv")
        s_hi = sem("s_hi")
        s_rest = sem("s_rest")
        s_mid = sem("s_mid")
        s_lo = sem("s_lo")
        s_s1 = [sem(f"s_s1{i}") for i in range(2)]
        s_s1_used = [sem(f"s_s1_used{i}") for i in range(2)]
        s_row_all = sem("s_row_all")
        s_h_all = sem("s_h_all")
        s_aused = sem("s_aused")
        s_acc_neg = sem("s_acc_neg")
        s_gsb = sem("s_gsb")
        s_x_last = sem("s_x_last")
        s_mask = sem("s_mask")
        s_amask = sem("s_amask")
        s_used = sem("s_used")
        s_acc = sem("s_acc")
        s_free = sem("s_free")
        s_exp = sem("s_exp")
        s_min = sem("s_min")
        s_var = sem("s_var")
        s_rs = sem("s_rs")
        s_x = sem("s_x")
        s_gw = sem("s_gw")
        s_batch = sem("s_batch")
        s_out = sem("s_out")

        N_B = 4 * NIG

        block2 = ctx.enter_context(nc.Block())

        @block2.sync
        def _(sp):
            def rows(dram, b, g):
                return dram.rearrange("(b g k p) c -> b g p k c", b=B, g=NIG, p=P)[bass.ds(b, 1), g].rearrange("o p k c -> (o p) k c")

            def load_x(b, g):
                sp.dma_start(xs[:, g * TPG:(g + 1) * TPG, :], rows(x1_dram, b, g)).then_inc(s_xl[g], 16)

            def load_masks(b):
                sp.dma_start(at[:, :, :, :].rearrange("p t j n -> p t (j n)"), at_dram.rearrange("(b t p) n -> b p t n", b=B, p=P)[bass.ds(b, 1)].rearrange("o p t n -> (o p) t n")).then_inc(s_atl, 16)

            def batch(b, more):
                for l in range(3):
                    H = heads[l]
                    for g in range(NIG):
                        sp.wait_ge(s_row_sb, b * 3 * NIG + l * NIG + g + 1)
                        sp.nop(nofuse=True)
                        sp.dma_start(s_dram[bass.ds(b * (3 * H2) + l * H2, H), g * IG:(g + 1) * IG],
                                     row_sb[g % 2][HPAD:HPAD + H, :]).then_inc(s_row_out[g % 2], 16)
                    for i in range(2):
                        sp.wait_ge(s_row_out[i], 16 * (b * (3 * NIG // 2) + (l + 1) * NIG // 2) + 16)
                        sp.nop(nofuse=True)
                    if H == 1:
                        sp.wait_ge(s_s1_used[0], 1)
                        sp.sem_inc(s_s1_used[0], -1)
                        sp.dma_start(s1b[0][:, 0:NIG, :].rearrange("p k n -> p (k n)"),
                                     s_dram[bass.ds(b * (3 * H2) + l * H2, 1), :].to_broadcast([P, N])).then_inc(s_s1[0], 16)
                    else:
                        with nc.sync.Fori(0, NIG) as g:
                            for i, (h0, h1) in enumerate(HEAD_GROUPS):
                                sp.wait_ge(s_s1_used[i], 1)
                                sp.sem_inc(s_s1_used[i], -1)
                                src = s_dram[bass.ds(b * (3 * H2) + l * H2 + h0, h1 - h0), bass.ds(g * IG, IG)]
                                sp.dma_start(s1b[i][:, 0:h1 - h0, :], src.partition_broadcast(P)).then_inc(s_s1[i], 16)
                for g in range(NIG):
                    sp.wait_ge(s_x_last, 1)
                    sp.sem_inc(s_x_last, -1)
                    sp.dma_start(rows(out_rows, b, g), xs[:, g * TPG:(g + 1) * TPG, :]).then_inc(s_out, 16)
                    sp.wait_ge(s_out, 16)
                    sp.sem_inc(s_out, -16)
                    if more:
                        load_x(b + 1, g)
                if more:
                    load_masks(b + 1)

            for g in range(NIG):
                load_x(0, g)
            load_masks(0)
            with nc.sync.Fori(0, B - 1) as b:
                batch(b, True)
            batch(B - 1, False)

        @block2.gpsimd
        def _(pool):
            with nc.gpsimd.Fori(0, B * N_B):
                pool.wait_ge(s_var, 1)
                pool.sem_inc(s_var, -1)
                nc.gpsimd.tensor_tensor(rs[:, :], mv[:, :, 1], minus_half[:, :], ALU.pow).then_inc(s_rs, 1)

        @block2.scalar
        def _(act):
            a = nc.scalar
            act.sem_inc(s_row_out[0], 16)
            act.sem_inc(s_row_out[1], 16)

            def copy_xT(g):
                for c in range(NC):
                    act.wait_ge(s_xT_ps, g * NC + c + 1)
                    if g >= 2:
                        act.wait_ge(s_h_ps, (g - 1) * TPG)
                    a.copy(xTc[g % 2][:, c, :], xt_ps[c][:, :]).then_inc(s_xT, 1)

            with nc.scalar.Fori(0, B) as b:
                for l in range(3):
                    H = heads[l]
                    bl = b * 3 + l

                    def copy_row(g):
                        act.wait_ge(s_row_out[g % 2], 16 * (bl * (NIG // 2) + g // 2 + 1))
                        act.nop(nofuse=True)
                        act.wait_ge(s_row_ps, g + 1)
                        src, dst = acc[g][HPAD:HPAD + H, :], row_sb[g % 2][HPAD:HPAD + H, :]
                        if l == 1:
                            a.activation(dst, src, ACT.Identity, bias=emb_col[HPAD:HPAD + H, :]).then_inc(s_row_sb, 1)
                        else:
                            a.copy(dst, src).then_inc(s_row_sb, 1)

                    if l == 0:
                        act.wait_ge(s_batch, 1)
                        act.sem_inc(s_batch, -1)
                    copy_xT(0)
                    for g in range(NIG):
                        if g < NIG - 1:
                            copy_xT(g + 1)
                        for k in range(TPG):
                            t = g * TPG + k
                            act.wait_ge(s_h_ps, t + 1)
                            if H == 1:
                                a.copy(h_ext[:, t, 0:C], pj_ps[t % 2][:, 0:C])
                            else:
                                a.copy(h_ext[:, t, :].rearrange("p (h w) -> p h w", w=HW)[:, :, 0:HD],
                                       pj_ps[t % 2][:, 0:C].rearrange("p (h d) -> p h d", d=HD))
                            a.copy(sc[:, t, 0:H], pj_ps[t % 2][:, C:C + H])
                            a.copy(sc[:, t, HPAD:HPAD + H], pj_ps[t % 2][:, C + H:C + 2 * H]).then_inc(s_h, 1)
                        if g > 0:
                            copy_row(g - 1)
                    act.drain().then_inc(s_h_all, 1)
                    copy_row(NIG - 1)
                    act.sem_inc(s_xT_ps, -NC * NIG)
                    act.sem_inc(s_h_ps, -NT)
                    act.sem_inc(s_row_ps, -NIG)
                    act.wait_ge(s_cols, 1)
                    act.sem_inc(s_cols, -1)
                    a.activation(v_pos[:, :, 0:H], dd[:, :, 0:H], ACT.Exp, bias=pos_bias[:, :])
                    a.activation(v_neg[:, :, 0:H], dd[:, :, 0:H], ACT.Exp, bias=neg_bias[:, :], scale=NEG_SLOPE)
                    a.activation(f_pos[:, :, 0:H], zz[:, :, 0:H], ACT.Exp)
                    a.activation(f_neg[:, :, 0:H], zp[:, :, 0:H], ACT.Exp, bias=row_bias[:, :], scale=-1.0).then_inc(s_w, 1)
                    act.drain()
                    for t in range(NT + 1):
                        if H > 1 and t < NT:
                            act.wait_ge(s_vv, t + 1)
                            a.copy(vb[:, t, 0, :], vv[t % VSLOTS][:, :]).then_inc(s_hi, 1)
                        if H > 1 and t > 0:
                            act.wait_ge(s_rest, t)
                            a.copy(vb[:, t - 1, 1, :], vv[(t - 1) % VSLOTS][:, :]).then_inc(s_mid, 1)
                        if H == 1 and t < NT:
                            a.activation(vp[:, t, 0, 0:FW], h_ext[:, t, 0:FW], ACT.Copy, scale=v_pos[:, t, 0:1])
                            a.activation(vp[:, t, 0, FW:2 * FW], h_ext[:, t, 0:FW], ACT.Copy, scale=v_neg[:, t, 0:1]).then_inc(s_hi, 1)
                    if l == 1:
                        act.sem_inc(s_rest, -NT)
                        act.sem_inc(s_vv, -NT)
                        def copy_masks(g, tiles):
                            for j in tiles:
                                act.wait_ge(s_aused, j + 1)
                                a.copy(aring[j % ARING][:, :].rearrange("p (k n) -> p k n", n=P),
                                       at[:, bass.ds(g * TPG, TPG), j, :]).then_inc(s_amask, 1)

                        def act_pass(g, more):
                            copy_masks(g, range(ARING, NT))
                            act.sem_inc(s_aused, -NT)
                            act.wait_ge(s_gw, 1)
                            act.sem_inc(s_gw, -1)
                            for k in range(TPG):
                                act.wait_ge(s_acc, k + 1)
                                a.copy(avs[:, k, :], acc[k][:, 0:H2 * HW])
                                a.copy(gsb[:, k, 0:G_SPLIT], acc[k][:, H2 * HW:H2 * HW + G_SPLIT]).then_inc(s_free, 1)
                            for k in range(TPG):
                                act.wait_ge(s_acc, TPG + k + 1)
                                a.copy(gsb[:, k, G_SPLIT:VW], acc[k][:, 0:VW - G_SPLIT]).then_inc(s_free, 1)
                            act.sem_inc(s_acc, -2 * TPG)
                            act.drain().then_inc(s_gsb, 1)
                            if more:
                                copy_masks(g + 1, range(ARING))
                            act.wait_ge(s_min, 1)
                            act.sem_inc(s_min, -1)
                            a.activation(ex[:, :, :], ee[:, :, :], ACT.Exp).then_inc(s_exp, 1)

                        copy_masks(0, range(ARING))
                        with nc.scalar.Fori(0, NIG - 1) as g:
                            act_pass(g, True)
                        act_pass(NIG - 1, False)
                    else:
                        with nc.scalar.Fori(0, NIG) as g:
                            for k in range(TPG):
                                act.wait_ge(s_acc, k + 1)
                                a.activation(gsb[:, k, 0:FW], acc[k][:, 0:FW], ACT.Copy, scale=f_pos[:, bass.ds(g * TPG + k, 1), 0]).then_inc(s_free, 1)
                            act.sem_inc(s_acc, -TPG)
                            act.drain().then_inc(s_gsb, 1)
                            if l == 2:
                                act.wait_ge(s_min, 1)
                                act.sem_inc(s_min, -1)
                                a.activation(ex[:, :, :], ee[:, :, :], ACT.Exp).then_inc(s_exp, 1)

        @block2.tensor
        def _(pe):
            pe.sem_inc(s_used, RING)
            pe.sem_inc(s_aused, ARING)
            pe.sem_inc(s_free, TPG)
            m = nc.tensor

            def transposes(l, g):
                if l == 0:
                    pe.wait_ge(s_xl[g], 16)
                    pe.sem_inc(s_xl[g], -16)
                for c in range(NC):
                    if g > 0:
                        pe.wait_ge(s_xT, (g - 1) * NC + c + 1)
                    for k in range(TPG):
                        mm = m.transpose(xt_ps[c][:, k * P:(k + 1) * P], xs[:, g * TPG + k, c * P:(c + 1) * P], ident[:, :])
                    mm.then_inc(s_xT_ps, 1)

            def unit(bank_cols, tiles, j, parts, rhs, first, last, done, nth):
                for k in range(TPG):
                    if first:
                        pe.wait_ge(s_free, nth * TPG + k + 1)
                    for part in range(parts):
                        mm = m.matmul(acc[k][:, bank_cols[0]:bank_cols[1]], tiles[:, k * P:(k + 1) * P], rhs(part),
                                      start=(first and part == 0), stop=(j == NT - 1 and part == parts - 1),
                                      skip_group_check=True)
                    if last and k < TPG - 1:
                        mm.then_inc(done, 1)
                return mm

            with nc.tensor.Fori(0, B) as b:
                for l in range(3):
                    H = heads[l]
                    if l > 0:
                        pe.wait_ge(s_x, NIG)
                        pe.sem_inc(s_x, -NIG)
                    def score_rows(g):
                        pe.wait_ge(s_h, (g + 1) * TPG)
                        for k in range(TPG):
                            mm = m.transpose(acc[g][0:HPAD + H, k * P:(k + 1) * P], sc[:, g * TPG + k, 0:HPAD + H], ident[:, :])
                        mm.then_inc(s_row_ps, 1)
                        pe.drain().then_inc(s_row_all, 1)

                    transposes(l, 0)
                    for g in range(NIG):
                        if g < NIG - 1:
                            transposes(l, g + 1)
                        pe.wait_ge(s_xT, (g + 1) * NC)
                        for k in range(TPG):
                            t = g * TPG + k
                            if t >= 2:
                                pe.wait_ge(s_h, t - 1)
                            for c in range(NC):
                                mm = m.matmul(pj_ps[t % 2][:, 0:C + 2 * H], xTc[g % 2][:, c, k * P:(k + 1) * P], w_ext[l][:, c, :],
                                              start=(c == 0), stop=(c == NC - 1))
                            mm.then_inc(s_h_ps, 1)
                        if g > 0:
                            score_rows(g - 1)
                    score_rows(NIG - 1)
                    pe.sem_inc(s_xT, -NC * NIG)
                    pe.sem_inc(s_h, -NT)
                    pe.wait_ge(s_mx, 1)
                    pe.sem_inc(s_mx, -1)
                    m.matmul(xt_ps[0][:, 0:H], mxb[0:H, :], ident[0:H, 0:H], start=True, stop=True).then_inc(s_mx_ps, 1)
                    pe.wait_ge(s_lo, NT)
                    pe.sem_inc(s_lo, -NT)

                    if l == 1:
                        with nc.tensor.Fori(0, NIG):
                            n = 0
                            for i, (h0, h1) in enumerate(HEAD_GROUPS):
                                for j in range(NT):
                                    if i == 0:
                                        pe.wait_ge(s_amask, j + 1)
                                        mm = unit((0, H2 * HW), aring[j % ARING], j, PARTS,
                                                  lambda part: vb[:, j, part, :].rearrange("p (h s w) -> p h s w", s=2, w=HW)[:, :, 1, :],
                                                  j == 0, False, None, i)
                                        mm.then_inc(s_aused, 1)
                                    for h in range(h0, h1):
                                        pe.wait_ge(s_mask, n + 1)
                                        col = (H2 * HW if i == 0 else 0) + (h - h0) * 2 * HW
                                        mm = unit((col, col + 2 * HW), ringb[n % RING], j, PARTS,
                                                  lambda part: vb[:, j, part, h * 2 * HW:(h + 1) * 2 * HW],
                                                  i > 0 and j == 0 and h == h0, j == NT - 1 and h == h1 - 1, s_acc, i)
                                        mm.then_inc(s_used, 1)
                                        n += 1
                                pe.drain().then_inc(s_acc, 1)
                            pe.sem_inc(s_free, -len(HEAD_GROUPS) * TPG)
                            pe.sem_inc(s_amask, -NT)
                            pe.sem_inc(s_mask, -NT * H2)
                    else:
                        with nc.tensor.Fori(0, NIG):
                            for br, done in enumerate((s_acc, s_acc_neg)):
                                for j in range(NT):
                                    n = br * NT + j
                                    pe.wait_ge(s_mask, n + 1)
                                    mm = unit((0, FW), ring[n % RING], j, 2,
                                              lambda part: vp[:, j, part, br * FW:(br + 1) * FW], j == 0, j == NT - 1, done, br)
                                    mm.then_inc(s_used, 1)
                                pe.drain().then_inc(done, 1)
                            pe.sem_inc(s_free, -2 * TPG)
                            pe.sem_inc(s_mask, -2 * NT)

        @block2.vector
        def _(dve):
            v = nc.vector
            dve.sem_inc(s_gw, 1)
            v.memset(sc[:, :, :], 0.0)
            dve.drain().then_inc(s_batch, 1)
            dve.sem_inc(s_s1_used[0], 1)
            dve.sem_inc(s_s1_used[1], 1)

            def moments(src):
                for k in range(TPG):
                    v.bn_stats(st[:, k, :], src[:, k, :])
                dve.drain()
                for k in range(TPG):
                    v.bn_aggr(mv[:, k, :], st[:, k, :])
                dve.drain()
                v.tensor_scalar(mv[:, :, 1], mv[:, :, 1], LN_EPS, None, ALU.add).then_inc(s_var, 1)

            def normalise(dst, src, meanwhile):
                moments(src)
                meanwhile()
                dve.wait_ge(s_rs, 1)
                dve.sem_inc(s_rs, -1)
                for k in range(TPG):
                    mm = v.tensor_scalar(dst(k), src[:, k, :], mv[:, k, 0:1], rs[:, k:k + 1], ALU.subtract, ALU.mult)
                return mm

            def elu_add(x_in):
                v.tensor_scalar(ee[:, :, :], yy[:, :, :], 0.0, None, ALU.min).then_inc(s_min, 1)
                dve.drain()
                v.tensor_tensor(yy[:, :, :], yy[:, :, :], ee[:, :, :], ALU.subtract)
                dve.drain()
                v.tensor_tensor(yy[:, :, :], yy[:, :, :], x_in, ALU.add)
                dve.drain()
                dve.wait_ge(s_exp, 1)
                dve.sem_inc(s_exp, -1)
                v.scalar_tensor_tensor(yy[:, :, :], ex[:, :, :], -1.0, yy[:, :, :], ALU.add, ALU.add)
                dve.drain()

            with nc.vector.Fori(0, B):
                for l in range(3):
                    H = heads[l]
                    dve.drain()
                    if H == 1:
                        v.memset(h_ext[:, :, C:C + 1], 1.0)
                        v.memset(h_ext[:, :, C + 1:C + 2], 0.0)
                    else:
                        hx = h_ext[:, :, :].rearrange("p t (h w) -> p (t h) w", w=HW)
                        v.memset(hx[:, :, HD:HD + 1], 1.0)
                        v.memset(hx[:, :, HD + 1:HD + 2], 0.0)
                    for g in range(NIG):
                        dve.wait_ge(s_row_all, 1)
                        dve.sem_inc(s_row_all, -1)
                        v.tensor_reduce(mx4[0:H, g:g + 1], acc[g][0:H, :], AX.X, ALU.max)
                    dve.drain()
                    v.tensor_reduce(mx[0:H, :], mx4[0:H, :], AX.X, ALU.max)
                    dve.drain()
                    v.tensor_copy(mxb[0:H, :], mx[0:H, 0:1].to_broadcast([H, P])).then_inc(s_mx, 1)
                    dve.wait_ge(s_h_all, 1)
                    dve.sem_inc(s_h_all, -1)
                    v.tensor_scalar(nsd[:, :, 0:H], sc[:, :, 0:H], -1.0, None, ALU.mult)
                    dve.wait_ge(s_mx_ps, 1)
                    dve.sem_inc(s_mx_ps, -1)
                    top_bc = xt_ps[0][:, 0:H].unsqueeze(1).to_broadcast([P, NT, H])
                    v.tensor_tensor(dd[:, :, 0:H], sc[:, :, 0:H], top_bc, ALU.subtract)
                    v.tensor_tensor(zz[:, :, 0:H], sc[:, :, HPAD:HPAD + H], top_bc, ALU.add)
                    dve.drain()
                    if l == 1:
                        v.tensor_tensor(zz[:, :, :], zz[:, :, :], emb_bc[:, :].unsqueeze(1).to_broadcast([P, NT, H2]), ALU.add)
                        dve.drain()
                    v.tensor_scalar(zp[:, :, 0:H], zz[:, :, 0:H], 1.0 - NEG_SLOPE, 0.0, ALU.mult, ALU.max)
                    dve.drain()
                    v.tensor_scalar(zz[:, :, 0:H], zz[:, :, 0:H], 1.0 - NEG_SLOPE, 0.0, ALU.mult, ALU.min).then_inc(s_cols, 1)
                    dve.wait_ge(s_w, 1)
                    dve.sem_inc(s_w, -1)
                    if H == 1:
                        for t in range(NT):
                            dve.wait_ge(s_hi, t + 1)
                            for s, w in enumerate((v_pos, v_neg)):
                                mm = v.scalar_tensor_tensor(vp[:, t, 1, s * FW:(s + 1) * FW], h_ext[:, t, 0:FW], w[:, t, 0:1],
                                                            vp[:, t, 0, s * FW:(s + 1) * FW].bitcast(F32), ALU.mult, ALU.subtract)
                            mm.then_inc(s_lo, 1)
                    else:
                        for t in range(NT + 2):
                            if t < NT:
                                he = h_ext[:, t, :].rearrange("p (h w) -> p h w", w=HW)
                                ve = vv[t % VSLOTS][:, :].rearrange("p (h s w) -> p h s w", s=2, w=HW)
                                v.tensor_tensor(ve[:, :, 0, :], he, v_pos[:, t, :].unsqueeze(2).to_broadcast([P, H2, HW]), ALU.mult)
                                v.tensor_tensor(ve[:, :, 1, :], he, v_neg[:, t, :].unsqueeze(2).to_broadcast([P, H2, HW]), ALU.mult).then_inc(s_vv, 1)
                            if 1 <= t <= NT:
                                dve.wait_ge(s_hi, t)
                                vt = vv[(t - 1) % VSLOTS]
                                v.tensor_tensor(vt[:, :], vt[:, :], vb[:, t - 1, 0, :], ALU.subtract).then_inc(s_rest, 1)
                            if t >= 2:
                                dve.wait_ge(s_mid, t - 1)
                                v.tensor_tensor(vb[:, t - 2, 2, :], vv[(t - 2) % VSLOTS][:, :], vb[:, t - 2, 1, :], ALU.subtract).then_inc(s_lo, 1)
                            dve.drain()
                        dve.sem_inc(s_mid, -NT)
                    dve.sem_inc(s_hi, -NT)
                    if l == 0:
                        dve.wait_ge(s_atl, 16)
                        dve.sem_inc(s_atl, -16)
                    if l == 1:
                        units = [(i, j, h) for i, (h0, h1) in enumerate(HEAD_GROUPS) for j in range(NT) for h in range(h0, h1)]

                        def take_scores(i):
                            dve.wait_ge(s_s1[i], 16)
                            dve.sem_inc(s_s1[i], -16)

                        def make_masks(g, n0, n1):
                            for n in range(n0, n1):
                                i, j, h = units[n]
                                dve.wait_ge(s_used, n + 1)
                                v.scalar_tensor_tensor(
                                    ringb[n % RING][:, :].rearrange("p (k n) -> p k n", n=P),
                                    s1b[i][:, h - HEAD_GROUPS[i][0], :].rearrange("p (k n) -> p k n", n=P),
                                    nsd[:, j, h:h + 1],
                                    at[:, bass.ds(g * TPG, TPG), j, :], ALU.is_gt, ALU.mult).then_inc(s_mask, 1)

                        def dve_pass(g, more):
                            make_masks(g, RING + 2 * SPARE, NT * HEAD_GROUPS[0][1])
                            dve.drain().then_inc(s_s1_used[0], 1)
                            take_scores(1)
                            make_masks(g, NT * HEAD_GROUPS[0][1], NT * H2)
                            dve.drain().then_inc(s_s1_used[1], 1)
                            dve.sem_inc(s_used, -NT * H2)
                            if more:
                                take_scores(0)
                                make_masks(g + 1, 0, RING)
                            dve.wait_ge(s_gsb, 1)
                            dve.sem_inc(s_gsb, -1)
                            gv = gsb[:, :, :].rearrange("p k (h s w) -> p (k h) s w", s=2, w=HW)
                            av = avs[:, :, :].rearrange("p k (h w) -> p (k h) w", w=HW)
                            tv = tot[:, :, :].rearrange("p k (h w) -> p (k h) w", w=HW)
                            def per_row(f):
                                return f[:, bass.ds(g * TPG, TPG), :].rearrange("p k h -> p (k h)").unsqueeze(2).to_broadcast([P, TPG * H2, HW])
                            v.tensor_tensor(av, av, gv[:, :, 1, :], ALU.subtract)
                            v.tensor_tensor(tv, gv[:, :, 0, :], per_row(f_pos), ALU.mult)
                            dve.drain()
                            v.tensor_tensor(av, av, per_row(f_neg), ALU.mult)
                            dve.drain()
                            v.tensor_tensor(tv, tv, av, ALU.add).then_inc(s_gw, 1)
                            dve.drain()
                            v.reciprocal(rden[:, :, :].rearrange("p k h -> p (k h)"), tv[:, :, HD])
                            dve.drain()
                            v.tensor_tensor(yy[:, :, :].rearrange("p k (h d) -> p (k h) d", d=HD), tv[:, :, 0:HD],
                                            rden[:, :, :].rearrange("p k h -> p (k h)").unsqueeze(2).to_broadcast([P, TPG * H2, HD]), ALU.mult)
                            dve.drain()
                            moments(yy)
                            for k in range(TPG):
                                v.scalar_tensor_tensor(yy[:, k, :], yy[:, k, :], mv[:, k, 0:1], gamma_bc[:, :], ALU.subtract, ALU.mult)
                            if more:
                                make_masks(g + 1, RING, RING + SPARE)
                            dve.drain()
                            dve.wait_ge(s_rs, 1)
                            dve.sem_inc(s_rs, -1)
                            for k in range(TPG):
                                v.scalar_tensor_tensor(yy[:, k, :], yy[:, k, :], rs[:, k:k + 1], beta_bc[:, :], ALU.mult, ALU.add)
                            dve.drain()
                            elu_add(xs[:, bass.ds(g * TPG, TPG), :])
                            normalise(lambda k: xs[:, bass.ds(g * TPG + k, 1), :].rearrange("p o c -> p (o c)"), yy,
                                      lambda: make_masks(g + 1, RING + SPARE, RING + 2 * SPARE) if more else None).then_inc(s_x, 1)

                        take_scores(0)
                        make_masks(0, 0, RING + 2 * SPARE)
                        with nc.vector.Fori(0, NIG - 1) as g:
                            dve_pass(g, True)
                        dve_pass(NIG - 1, False)
                    else:
                        dve.wait_ge(s_s1[0], 16)
                        dve.sem_inc(s_s1[0], -16)
                        def make_masks(g, n0, n1):
                            s1 = s1b[0][:, bass.ds(g, 1), :].rearrange("p o (k n) -> p (o k) n", n=P)
                            for n in range(n0, n1):
                                br, j = divmod(n, NT)
                                dve.wait_ge(s_used, n + 1)
                                v.scalar_tensor_tensor(
                                    ring[n % RING][:, :].rearrange("p (k n) -> p k n", n=P), s1, nsd[:, j, 0:1],
                                    at[:, bass.ds(g * TPG, TPG), j, :], ALU.is_le if br else ALU.is_gt, ALU.mult).then_inc(s_mask, 1)

                        def dve_pass(g, more):
                            make_masks(g, RING + SPARE, 2 * NT)
                            dve.sem_inc(s_used, -2 * NT)
                            if more:
                                make_masks(g + 1, 0, RING)
                            dve.wait_ge(s_gsb, 1)
                            dve.sem_inc(s_gsb, -1)
                            for k in range(TPG):
                                dve.wait_ge(s_acc_neg, k + 1)
                                v.scalar_tensor_tensor(tot[:, k, 0:FW], acc[k][:, 0:FW], f_neg[:, bass.ds(g * TPG + k, 1), 0],
                                                       gsb[:, k, 0:FW], ALU.mult, ALU.add).then_inc(s_free, 1)
                            dve.sem_inc(s_acc_neg, -TPG)
                            dve.drain()
                            v.reciprocal(rden[:, :, 0], tot[:, :, C])
                            dve.drain()
                            xg = xs[:, bass.ds(g * TPG, TPG), :]
                            if l == 0:
                                for k in range(TPG):
                                    v.scalar_tensor_tensor(yy[:, k, :], tot[:, k, 0:C], rden[:, k, 0:1],
                                                           xs[:, bass.ds(g * TPG + k, 1), :].rearrange("p o c -> p (o c)"), ALU.mult, ALU.add)
                            else:
                                for k in range(TPG):
                                    v.tensor_scalar(yy[:, k, :], tot[:, k, 0:C], rden[:, k, 0:1], None, ALU.mult)
                            dve.drain()
                            if l == 2:
                                elu_add(xg)
                            normalise(lambda k: xs[:, bass.ds(g * TPG + k, 1), :].rearrange("p o c -> p (o c)"), yy,
                                      lambda: make_masks(g + 1, RING, RING + SPARE) if more else None).then_inc(s_x_last if l == 2 else s_x, 1)

                        make_masks(0, 0, RING + SPARE)
                        with nc.vector.Fori(0, NIG - 1) as g:
                            dve_pass(g, True)
                        dve_pass(NIG - 1, False)
                        dve.drain().then_inc(s_s1_used[0], 1)
                dve.drain().then_inc(s_batch, 1)


_INS = ['x', 'adj', 'L0_gnn_W', 'L0_gnn_b', 'L1_gnn_W', 'L1_gnn_a', 'L2_gnn_W', 'L2_gnn_a1', 'L2_gnn_a2',
        'L2_gnn_edge_emb', 'L2_gnn_ln_gamma', 'L2_gnn_ln_beta', 'L3_gnn_W', 'L3_gnn_a']


def kernel(**inputs):
    import numpy as _np
    import concourse.bacc as _bacc
    from concourse import mybir as _mybir
    from concourse.bass_utils import run_bass_kernel_spmd as _run

    nc = _bacc.Bacc("TRN2", target_bir_lowering=False, num_devices=1)
    arrays, args = {}, []
    for name in _INS:
        a = _np.ascontiguousarray(inputs[name])
        arrays[f"in_{name}_dram"] = a
        args.append(nc.dram_tensor(f"in_{name}_dram", a.shape, _mybir.dt.from_np(a.dtype), kind="ExternalInput").ap())
    shape = inputs['x'].shape
    args.append(nc.dram_tensor("out_dram", shape, _mybir.dt.float32, kind="ExternalOutput").ap())
    four_layer_graph_kernel(nc, *args)
    r = _run(nc, [arrays], core_ids=[0])
    return r.results[0]["out_dram"]
```
